# Optimizing a Trainium2 kernel written in Bass

```python
import numpy as np
import jax
import jax.numpy as jnp

def _softmax(x, axis=-1):
    return jax.nn.softmax(x, axis=axis)

def _gelu(x):
    return jax.nn.gelu(x, approximate=True)

def _silu(x):
    return jax.nn.silu(x)

def _sigmoid(x):
    return jax.nn.sigmoid(x)

def _layernorm(x, axis=-1, eps=1e-05):
    m = jnp.mean(x, axis=axis, keepdims=True)
    v = jnp.var(x, axis=axis, keepdims=True)
    return (x - m) / jnp.sqrt(v + eps)

def _scatter_add(tgt, idx, src, axis=0):
    return tgt.at[idx].add(src)

def _segment_sum(src, seg, n):
    return jax.ops.segment_sum(src, seg, n)
kernel_name = 'mk_prb_d1_jaxref_r8_962966'

def setup_inputs(seed: int=0):
    np.random.seed(seed)
    _w = jnp.asarray

    def _L0_attn_setup():
        import jax, jax.numpy as jnp
        import numpy as np
        import math
        D_MODEL, N_HEADS, D_K, D_C, D_HR = (128, 8, 128, 32, 32)
        B, S = (4, 256)
        key = jax.random.key(seed)
        ks = jax.random.split(key, 17)

        def lin(k, fan_in, fan_out):
            lim = 1.0 / math.sqrt(fan_in)
            kw, kb = jax.random.split(k)
            W = jax.random.uniform(kw, (fan_in, fan_out), jnp.float32, -lim, lim)
            b = jax.random.uniform(kb, (fan_out,), jnp.float32, -lim, lim)
            return (W, b)
        W_DQ, b_DQ = lin(ks[0], D_MODEL, D_C)
        W_UQ, b_UQ = lin(ks[1], D_C, N_HEADS * D_K)
        W_DKV, b_DKV = lin(ks[2], D_MODEL, D_C)
        W_UK, b_UK = lin(ks[3], D_C, N_HEADS * D_K)
        W_UV, b_UV = lin(ks[4], D_C, N_HEADS * D_K)
        W_QR, b_QR = lin(ks[5], D_C, N_HEADS * D_HR)
        W_KR, b_KR = lin(ks[6], D_MODEL, D_HR)
        W_O, b_O = lin(ks[7], N_HEADS * D_K, D_MODEL)
        h_t = jax.random.normal(ks[8], (B, S, D_MODEL), jnp.float32)
        return {'h_t': h_t, 'W_DQ': W_DQ, 'b_DQ': b_DQ, 'W_UQ': W_UQ, 'b_UQ': b_UQ, 'W_DKV': W_DKV, 'b_DKV': b_DKV, 'W_UK': W_UK, 'b_UK': b_UK, 'W_UV': W_UV, 'b_UV': b_UV, 'W_QR': W_QR, 'b_QR': b_QR, 'W_KR': W_KR, 'b_KR': b_KR, 'W_O': W_O, 'b_O': b_O}
    _L0_attn_in = _L0_attn_setup()

    def _L0_ffn_setup():
        import jax, jax.numpy as jnp
        import numpy as np
        B, S, D, E, F, TOP_K = (4, 256, 128, 8, 512, 2)
        key = jax.random.key(seed)
        k0, k1, k2, k3 = jax.random.split(key, 4)
        init = lambda k, shape, fan: (jax.random.normal(k, shape, jnp.float32) / np.sqrt(fan)).astype(jnp.float32)
        return {'x': jax.random.normal(k0, (B, S, D), jnp.float32), 'gate_w': init(k1, (D, E), D), 'w1': init(k2, (E, D, F), D), 'b1': jnp.zeros((E, F), jnp.float32), 'w2': init(k3, (E, F, D), F), 'b2': jnp.zeros((E, D), jnp.float32)}
    _L0_ffn_in = _L0_ffn_setup()
    _d = {'L0_attn_h_t': _L0_attn_in['h_t'], 'L0_attn_W_DQ': _L0_attn_in['W_DQ'], 'L0_attn_b_DQ': _L0_attn_in['b_DQ'], 'L0_attn_W_UQ': _L0_attn_in['W_UQ'], 'L0_attn_b_UQ': _L0_attn_in['b_UQ'], 'L0_attn_W_DKV': _L0_attn_in['W_DKV'], 'L0_attn_b_DKV': _L0_attn_in['b_DKV'], 'L0_attn_W_UK': _L0_attn_in['W_UK'], 'L0_attn_b_UK': _L0_attn_in['b_UK'], 'L0_attn_W_UV': _L0_attn_in['W_UV'], 'L0_attn_b_UV': _L0_attn_in['b_UV'], 'L0_attn_W_QR': _L0_attn_in['W_QR'], 'L0_attn_b_QR': _L0_attn_in['b_QR'], 'L0_attn_W_KR': _L0_attn_in['W_KR'], 'L0_attn_b_KR': _L0_attn_in['b_KR'], 'L0_attn_W_O': _L0_attn_in['W_O'], 'L0_attn_b_O': _L0_attn_in['b_O'], 'L0_ffn_gate_w': _L0_ffn_in['gate_w'], 'L0_ffn_w1': _L0_ffn_in['w1'], 'L0_ffn_b1': _L0_ffn_in['b1'], 'L0_ffn_w2': _L0_ffn_in['w2'], 'L0_ffn_b2': _L0_ffn_in['b2']}
    _x0 = _d['L0_attn_h_t']
    _d['L0_attn_h_t'] = jax.random.normal(jax.random.fold_in(jax.random.key(seed), 1), (4, 1024, 128), dtype=_x0.dtype)
    del _x0
    return _d

def reference(L0_attn_h_t, L0_attn_W_DQ, L0_attn_b_DQ, L0_attn_W_UQ, L0_attn_b_UQ, L0_attn_W_DKV, L0_attn_b_DKV, L0_attn_W_UK, L0_attn_b_UK, L0_attn_W_UV, L0_attn_b_UV, L0_attn_W_QR, L0_attn_b_QR, L0_attn_W_KR, L0_attn_b_KR, L0_attn_W_O, L0_attn_b_O, L0_ffn_gate_w, L0_ffn_w1, L0_ffn_b1, L0_ffn_w2, L0_ffn_b2):

    def _L0_attn_ref(h_t, W_DQ, b_DQ, W_UQ, b_UQ, W_DKV, b_DKV, W_UK, b_UK, W_UV, b_UV, W_QR, b_QR, W_KR, b_KR, W_O, b_O):
        import jax, jax.numpy as jnp
        import numpy as np
        import math
        D_MODEL, N_HEADS, D_K, D_C, D_HR = (128, 8, 128, 32, 32)
        B, S = (4, 256)
        b, s, _ = h_t.shape
        c_q = h_t @ W_DQ + b_DQ
        c_kv = h_t @ W_DKV + b_DKV
        q_c = (c_q @ W_UQ + b_UQ).reshape(b, s, N_HEADS, D_K).transpose(0, 2, 1, 3)
        k_c = (c_kv @ W_UK + b_UK).reshape(b, s, N_HEADS, D_K).transpose(0, 2, 1, 3)
        v_c = (c_kv @ W_UV + b_UV).reshape(b, s, N_HEADS, D_K).transpose(0, 2, 1, 3)
        q_r = (c_q @ W_QR + b_QR).reshape(b, s, N_HEADS, D_HR).transpose(0, 2, 1, 3)
        k_r = (h_t @ W_KR + b_KR)[:, None, :, :]
        k_r = jnp.broadcast_to(k_r, (b, N_HEADS, s, D_HR))
        q = jnp.concatenate([q_c, q_r], axis=-1)
        k = jnp.concatenate([k_c, k_r], axis=-1)
        scale = 1.0 / math.sqrt(D_K + D_HR)
        scores = jnp.einsum('bhsd,bhtd->bhst', q, k) * scale
        attn = jax.nn.softmax(scores, axis=-1)
        o = jnp.einsum('bhst,bhtd->bhsd', attn, v_c)
        o = o.transpose(0, 2, 1, 3).reshape(b, s, N_HEADS * D_K)
        return o @ W_O + b_O

    def _L0_ffn_ref(x, gate_w, w1, b1, w2, b2):
        import jax, jax.numpy as jnp
        import numpy as np
        B, S, D, E, F, TOP_K = (4, 256, 128, 8, 512, 2)
        b, s, d = x.shape
        e = gate_w.shape[1]
        xf = x.reshape(-1, d)
        t = xf.shape[0]
        logits = xf @ gate_w
        top_w, top_idx = jax.lax.top_k(logits, TOP_K)
        top_w = jax.nn.softmax(top_w.astype(jnp.float32), axis=-1).astype(x.dtype)
        combine = jnp.zeros((t, e), x.dtype).at[jnp.arange(t)[:, None], top_idx].add(top_w)
        h = jax.nn.gelu(jnp.einsum('td,edf->tef', xf, w1) + b1, approximate=False)
        y = jnp.einsum('tef,efd->ted', h, w2) + b2
        out = jnp.einsum('ted,te->td', y, combine)
        return out.reshape(b, s, d)
    x = L0_attn_h_t
    xn = _layernorm(x, axis=-1)
    x = x + _L0_attn_ref(xn, L0_attn_W_DQ, L0_attn_b_DQ, L0_attn_W_UQ, L0_attn_b_UQ, L0_attn_W_DKV, L0_attn_b_DKV, L0_attn_W_UK, L0_attn_b_UK, L0_attn_W_UV, L0_attn_b_UV, L0_attn_W_QR, L0_attn_b_QR, L0_attn_W_KR, L0_attn_b_KR, L0_attn_W_O, L0_attn_b_O) + _L0_ffn_ref(xn, L0_ffn_gate_w, L0_ffn_w1, L0_ffn_b1, L0_ffn_w2, L0_ffn_b2)
    return x

_drawn_inputs = setup_inputs


def setup_inputs(seed=0):
    import zlib

    import numpy as np

    out = dict(_drawn_inputs(seed))
    spreads = {'L0_ffn_b1': (0.0, 0.8), 'L0_ffn_b2': (0.0, 0.72)}
    factors = {'L0_attn_W_DQ': 8.0,
     'L0_attn_b_DQ': 8.0,
     'L0_attn_W_UQ': 8.0,
     'L0_attn_b_UQ': 8.0,
     'L0_attn_W_DKV': 8.0,
     'L0_attn_b_DKV': 4.722,
     'L0_attn_W_UK': 8.0,
     'L0_attn_b_UK': 64.0,
     'L0_attn_W_UV': 3.744,
     'L0_attn_W_QR': 8.0,
     'L0_attn_b_QR': 8.0,
     'L0_attn_W_KR': 8.0,
     'L0_attn_b_KR': 64.0,
     'L0_attn_b_O': 19.569,
     'L0_attn_b_UV': 6.191}
    for name, (base, spread) in spreads.items():
        noise = np.random.default_rng([zlib.crc32(name.encode()), seed]).standard_normal(out[name].shape)
        drawn = base * np.exp(spread * noise) if base else spread * noise
        out[name] = jnp.asarray(drawn.astype(out[name].dtype))
    for name, factor in factors.items():
        out[name] = (out[name] * factor).astype(out[name].dtype)
    return out
```

```python
import concourse.bass as bass
from concourse import mybir
from contextlib import ExitStack

FP32 = mybir.dt.float32
FP32R = mybir.dt.float32r
U32 = mybir.dt.uint32
I32 = mybir.dt.int32
ALU = mybir.AluOpType
ACT = mybir.ActivationFunctionType
AX = mybir.AxisListType

P = 128
B, S, D = 4, 1024, 128
H, DK, DC, DR = 8, 128, 32, 32
NT = B * S // P
QC = 512
NC = S // QC
KT = S // P
NQ = B * S // QC
SCALE = 1.0 / (DK + DR) ** 0.5
EPS = 1e-5
KD = DC + DR
ROW_QB = KD
ROW_MAX = KD + 1
CW = 64
ONE = DC
OW = D + 1
NHEADS = B * H
F, E, TOPK = 512, 8, 2
FT = F // P
NTOK = B * S
SLOTS = 256
NTILES = (NTOK * TOPK + E * (SLOTS - 1)) // SLOTS
PAIRS = NHEADS // 2
SPLIT = 7
DISPATCH = 8
COMBINE = NT // (PAIRS - SPLIT - 1)


def moe_transformer_layer(nc, x, wdq, bdq, wuq, buq, wdkv, bdkv, wuk, buk, wuv, buv, wqr, bqr,
                          wkr, bkr, wo, bo, gate, w1, w2, b12, out):
    with ExitStack() as ctx:
        def sb(name, shape, dt=FP32):
            return ctx.enter_context(nc.sbuf_tensor(name, shape, dt))

        def sem(name):
            return ctx.enter_context(nc.semaphore(name))

        xn = sb("xn", [P, NT, D])
        acc = sb("acc", [P, NT, D])
        xn_st = sb("xn_st", [P, 2, 4, D])
        xT_st = sb("xT_st", [P, 2, QC])
        xq = sb("xq", [P, B * S], FP32R)
        k_hh = sb("k_hh", [P, B * S], FP32R)
        k_h1 = sb("k_h1", [P, B * S], FP32R)
        k_l1 = sb("k_l1", [P, B * S], FP32R)
        ckv = sb("ckv", [P, NT, CW])
        logits = sb("logits", [P, NT, H])
        wq_abs = sb("wq_abs", [P, H, KD + 1], FP32R)
        wvo = sb("wvo", [P, H, OW])
        ident = sb("ident", [P, P])
        b_k = sb("b_k", [P, 1])
        b_cq = sb("b_cq", [P, 1])
        w_k2 = sb("w_k2", [P, P])
        w_cq = sb("w_cq", [P, P])
        w_cg = sb("w_cg", [P, DC + H])
        bkv_bc = sb("bkv_bc", [P, DC])
        bo_bc = sb("bo_bc", [P, D])
        wq_cur = sb("wq_cur", [P, 2, 2 * P], FP32R)
        k_hh_cur = sb("k_hh_cur", [P, 2, S], FP32R)
        k_l1_cur = sb("k_l1_cur", [P, 2, S], FP32R)
        ckv_cur = sb("ckv_cur", [P, 2, KT * CW])
        q_hl = sb("q_hl", [P, 2, S], FP32R)
        q_h1 = sb("q_h1", [P, 2, S], FP32R)
        mcol = sb("mcol", [P, 2, KT])
        mrow = sb("mrow", [4, 2, P], FP32R)
        ctx_sb = sb("ctx_sb", [P, 2, QC])
        rsum = sb("rsum", [P, 2, 2])
        probs = sb("probs", [P, 4, 2 * QC])
        stat = sb("stat", [P, NT, 6])
        mv = sb("mv", [P, NT, 2])
        rstd = sb("rstd", [P, 4, NT])

        first_w = sb("first_w", [P, 2, NT])
        slot_of = sb("slot_of", [P, 2, NT], U32)
        expert_of = sb("expert_of", [P, NTILES], U32)
        upper = sb("upper", [P, P])
        ones = sb("ones", [P, P])
        falling = sb("falling", [P, E])
        tile_no = sb("tile_no", [P, NTILES])
        slot_st = sb("slot_st", [P, 2 * COMBINE, 1], U32)
        row_st = sb("row_st", [P, 2, D])
        fetched = sb("fetched", [P, 2 * COMBINE, D])

        xs_dram = nc.dram_tensor("x_sorted", (NTILES * SLOTS, D), FP32).ap()
        ys_dram = nc.dram_tensor("y_sorted", (NTILES * SLOTS, D), FP32).ap()

        ps = ctx.enter_context(nc.psum_tensor("ps", [P, 8 * 512], FP32))
        sc = [ps[:, 1024 * i:1024 * (i + 1)] for i in range(2)]
        mx = ps[:, 2048:3072]
        cx = ps[:, 3072:3584]
        aux = ps[:, 3584:4096]

        uq33 = probs[0:33, 0, :]
        uk33 = probs[0:33, 1, :]
        uv33 = probs[0:33, 2, :]
        wo_sb = sb("wo_sb", [P, H, D])
        prep = sb("prep", [P, 3, H * P])
        uq3, uv2, fmat = prep[:, 0, :], prep[:, 1, :], prep[:, 2, :]
        w1_t = prep[:, 0:1, :].rearrange("p a (b f) -> p (a b) f", b=2)
        w2_t = prep[:, 1:2, :].rearrange("p a (b f) -> p (a b) f", b=2)
        h_t = [prep[:, 2, :], wo_sb[:, :, :].rearrange("p h d -> p (h d)")]
        xg = xn_st[:, :, 0:2, :]
        y_out = xn_st[:, :, 2:4, :]
        xgT = xT_st[:, :, 0:SLOTS]
        yT = xT_st[:, 0, SLOTS:2 * SLOTS]
        b12_t = sb("b12_t", [P, 2, FT + 1])
        ukT = ctx_sb[:, 0, 0:H * 33]
        qr98 = ctx_sb[:, 1, 0:H * DR]
        hi_mask, lo_mask = rsum[:, 0, 0:1], rsum[:, 0, 1:2]

        d_x = [sem(f"x_loaded{i}") for i in range(4)]
        d_w = sem("weights_loaded")
        d_k = sem("key_weights_loaded")
        ident_made = sem("ident_made")
        consts_made = sem("consts_made")
        pool_done = sem("pool_done")
        dve_done = sem("dve_done")
        var_ready = sem("var_ready")
        std_ready = sem("std_ready")
        xn_ready = sem("xn_ready")
        wT_ready = sem("wT_ready")
        wT_copied = sem("wT_copied")
        prod_ready = sem("prod_ready")
        wq_made = sem("wq_made")
        wvo_made = sem("wvo_made")
        xT_ready = sem("xT_ready")
        xT_copied = sem("xT_copied")
        k_ready = sem("k_ready")
        cq_ready = sem("cq_ready")
        cg_ready = sem("cg_ready")
        k_copied = sem("k_copied")
        k_low = sem("k_low")
        cq_copied = sem("cq_copied")
        cq_low = sem("cq_low")
        c_copied = sem("c_copied")
        k_top = sem("k_top")
        bo_added = sem("bo_added")
        xn_kept = sem("xn_kept")
        zeros_stored = sem("zeros_stored")
        gap_ready = sem("gap_ready")
        gap_exp = sem("gap_exp")
        chosen = sem("chosen")
        counted = sem("counted")
        routed = sem("routed")
        staged = sem("staged")
        pool_waited = sem("pool_waited")
        rows_sent_k = [sem(f"rows_sent{k}") for k in range(TOPK)]
        rows_fetched = sem("rows_fetched")
        rows_added = sem("rows_added")
        half_added = sem("half_added")
        x_in = [sem(f"slots_loaded{i}") for i in range(2)]
        w1_in = [sem(f"w1_loaded{i}") for i in range(2)]
        w2_in = [sem(f"w2_loaded{i}") for i in range(2)]
        b_in = [sem(f"expert_biases_loaded{i}") for i in range(2)]
        xgT_ready = sem("xgT_ready")
        xgT_copied = sem("xgT_copied")
        hidden_ready = sem("hidden_ready")
        hidden_done = sem("hidden_done")
        yT_ready = sem("yT_ready")
        yT_copied = sem("yT_copied")
        y_ready = sem("y_ready")
        y_copied = sem("y_copied")
        y_stored = [sem(f"y_stored{i}") for i in range(2)]
        scores_ready = sem("scores_ready")
        probs_ready = sem("probs_ready")
        context_added = sem("context_added")
        context_copied = sem("context_copied")
        max_ready = sem("max_ready")
        max_done = sem("max_done")
        maxT_ready = sem("maxT_ready")
        mrow_ready = sem("mrow_ready")
        mrow_moved = [sem(f"mrow_moved{c}") for c in range(2)]
        q_ready = sem("q_ready")
        q_hi_done = sem("q_hi_done")
        q_lo_done = sem("q_lo_done")
        q_h1_done = sem("q_h1_done")
        head_out_ready = sem("head_out_ready")
        recip_done = sem("recip_done")
        head_out_added = sem("head_out_added")
        keys_current = sem("keys_current")
        wq_current = sem("wq_current")
        out_stored = sem("out_stored")

        block = ctx.enter_context(nc.Block())

        xv = x.rearrange("b (t p) d -> p (b t) d", p=P)
        ov = out.rearrange("b (t p) d -> p (b t) d", p=P)

        def col(v):
            return v.rearrange("(p a) -> p a", a=1)

        def row(v):
            return v.rearrange("(a p) -> a p", a=1)

        def run_heads(eng, head, experts):
            head(0, 0, first=True)
            head(1, 1, second=True)
            with eng.Fori(1, SPLIT) as j:
                head(j * 2, 0)
                head(j * 2 + 1, 1)
            experts()
            with eng.Fori(SPLIT, PAIRS - 1) as j:
                head(j * 2, 0, late=j - SPLIT)
                head(j * 2 + 1, 1, late=j - SPLIT)
            head(NHEADS - 2, 0, ahead=1)
            head(NHEADS - 1, 1, ahead=0)

        def over_tiles(eng, tile):
            tile(0, 0)
            tile(1, 1)
            with eng.Fori(1, NTILES // 2) as j:
                tile(j * 2, 0)
                tile(j * 2 + 1, 1)
            tile(NTILES - 1, 0)

        NLOADS = 7 + 8 + 3 + 9 + 2 + 1

        @block.sync
        def _(sp):
            for i in range(4):
                sp.dma_start(acc[:, i * 8:(i + 1) * 8, :], xv[:, i * 8:(i + 1) * 8, :]).then_inc(d_x[i], 16)
            n = [0]

            def load(dst, src):
                sp.dma_start(dst, src).then_inc(d_w, 16)
                n[0] += 1
            load(uq33[0:DC, :], wuq)
            load(uq33[DC:DC + 1, :], row(buq))
            load(uk33[0:DC, :], wuk)
            load(uk33[DC:DC + 1, :], row(buk))
            load(uv33[0:DC, :], wuv)
            load(uv33[DC:DC + 1, :], row(buv))
            load(wo_sb[:, :, :], wo.rearrange("(h k) d -> k h d", k=DK))
            for g in range(2):
                load(w_k2[:, g * KD:g * KD + DC], wdkv)
                load(w_k2[:, g * KD + DC:(g + 1) * KD], wkr)
                load(b_k[g * KD:g * KD + DC, :], col(bdkv))
                load(b_k[g * KD + DC:(g + 1) * KD, :], col(bkr))
            load(w_cg[:, 0:DC], wdkv)
            load(w_cg[:, DC:DC + H], gate)
            load(bkv_bc[:, :], bdkv.partition_broadcast(P))
            load(bo_bc[:, :], bo.partition_broadcast(P))
            sp.wait_ge(consts_made, 1)
            for g in range(3):
                load(w_cq[:, g * DC:(g + 1) * DC], wdq)
                load(b_cq[g * DC:(g + 1) * DC, :], col(bdq))
                load(qr98[g * DC:(g + 1) * DC, :], wqr)
            load(qr98[96:97, :], row(bqr))
            load(qr98[97:98, :], row(bqr))
            assert n[0] == NLOADS, n[0]

            def move_max(n, c, parity):
                sp.wait_ge(mrow_ready, n * 2 + (c + 1))
                sp.dma_start(q_h1[ROW_MAX:ROW_MAX + 1, parity, c * QC:(c + 1) * QC].bitcast(FP32),
                             mrow[:, c, :].bitcast(FP32)).then_inc(mrow_moved[c], 16)

            def load_tile(i, parity):
                first = isinstance(i, int) and i < 2
                e = sp.value_load(expert_of[0:1, bass.ds(i, 1)], min_val=0, max_val=E - 1)
                if not first:
                    sp.wait_ge(xgT_ready, i - 1)
                sp.dma_start(xg[:, parity, :, :],
                             xs_dram[bass.ds(i * SLOTS, SLOTS), :].rearrange("(a p) d -> p a d", p=P))\
                    .then_inc(x_in[parity], 16)
                if not first:
                    sp.wait_ge(hidden_ready, i * FT - FT)
                sp.dma_start(w1_t[:, parity, :], w1[bass.ds(e, 1), :, :].rearrange("a d f -> d (a f)"))\
                    .then_inc(w1_in[parity], 16)
                if not first:
                    sp.wait_ge(yT_copied, i - 1)
                sp.dma_start(w2_t[:, parity, :].rearrange("p (a d) -> p a d", a=FT),
                             w2[bass.ds(e, 1), :, :].rearrange("o (a p) d -> p (o a) d", p=P))\
                    .then_inc(w2_in[parity], 16)
                sp.dma_start(b12_t[:, parity, :], b12[bass.ds(e, 1), :, :].rearrange("o p a -> p (o a)"))\
                    .then_inc(b_in[parity], 16)

            sp.wait_ge(consts_made, 4)
            sp.dma_start(xs_dram.rearrange("(t p) d -> p t d", p=P),
                         row_st[:, 0, :].unsqueeze(1).to_broadcast([P, NTILES * SLOTS // P, D])).then_inc(zeros_stored, 16)

            def move_pair(j):
                for parity in range(2):
                    for c in range(NC):
                        move_max(j * 2 + parity, c, parity)

            with sp.Fori(0, SPLIT) as j:
                move_pair(j)
            move_max(2 * SPLIT, 0, 0)
            for k in range(TOPK):
                sp.wait_ge(rows_sent_k[k], 16 * NT)
            sp.wait_ge(routed, 1)
            over_tiles(sp, load_tile)
            move_max(2 * SPLIT, 1, 0)
            move_max(2 * SPLIT + 1, 0, 1)
            move_max(2 * SPLIT + 1, 1, 1)
            with sp.Fori(SPLIT + 1, PAIRS) as j:
                move_pair(j)
            sp.wait_ge(head_out_added, 4 * NHEADS)
            sp.wait_ge(rows_added, PAIRS - SPLIT - 1)
            sp.dma_start(ov, acc[:, :, :]).then_inc(out_stored, 16)
            sp.wait_ge(out_stored, 16)

        @block.gpsimd
        def _(pool):
            steps = [0]

            def link(ins):
                steps[0] += 1
                ins.then_inc(pool_done, 1)
                pool.wait_ge(pool_done, steps[0])
            link(pool.memset(w_cq[:, :], 0.0))
            link(pool.memset(b_cq[96:128, :], 1.0))
            pool.memset(ctx_sb[:, 1, 0:H * DR], 0.0).then_inc(consts_made, 1)
            link(pool.memset(ident[:, :], 0.0))
            pool.affine_select(out=ident[:, :], in_=ident[:, :], compare_op=ALU.not_equal, fill=1.0,
                               base=0, pattern=[[-1, P]], channel_multiplier=1).then_inc(ident_made, 1)
            pool.memset(prep[:, 0:2, :], 0.0).then_inc(consts_made, 1)
            link(pool.memset(wq_cur[:, :, :].bitcast(FP32), 0.0))
            link(pool.memset(k_h1[KD:P, :].bitcast(FP32), 0.0))
            link(pool.memset(k_l1[KD:P, :].bitcast(FP32), 0.0))
            link(pool.memset(k_h1[KD:KD + 1, :].bitcast(FP32), 1.0))
            link(pool.memset(k_l1[KD:KD + 2, :].bitcast(FP32), 1.0))
            link(pool.memset(ckv[:, :, DC:CW], 0.0))
            pool.memset(ckv[:, :, ONE:ONE + 1], 1.0).then_inc(consts_made, 1)
            pool.memset(row_st[:, 0, :], 0.0).then_inc(consts_made, 1)
            link(pool.memset(ones[:, :], 1.0))
            pool.affine_select(out=upper[:, :], in_=ones[:, :], compare_op=ALU.is_gt, fill=0.0,
                               base=0, pattern=[[1, P]], channel_multiplier=-1)
            pool.iota(falling[:, :], pattern=[[-1, E]], base=E, channel_multiplier=0,
                      allow_small_or_imprecise_dtypes=True)
            pool.iota(tile_no[:, :], pattern=[[1, NTILES]], base=0, channel_multiplier=0,
                      allow_small_or_imprecise_dtypes=True).then_inc(consts_made, 1)
            pool.wait_ge(d_w, 16 * NLOADS)
            with pool.Fori(0, NQ // 2) as j:
              for par in range(2):
                ck = j * 2 + par
                pool.wait_ge(consts_made, 5)
                pool.wait_ge(xn_ready, ck + 1)
                pool.tensor_copy(xn[:, bass.ds(ck * 4, 4), :], xn_st[:, par, :, :]).then_inc(xn_kept, 1)
                a = acc[:, bass.ds(ck * 4, 4), :]
                pool.tensor_tensor(a, a, bo_bc[:, :].unsqueeze(1).to_broadcast([P, 4, D]), ALU.add)\
                    .then_inc(bo_added, 1)

            def query_weights(n, parity, first=False):
                pool.wait_ge(wq_made, 1)
                if not first:
                    pool.wait_ge(q_ready, n * 4 - 4)
                src = wq_abs[:, bass.ds(n % H, 1), :].rearrange("p a k -> p (a k)")
                pool.tensor_copy(wq_cur[:, parity, 0:KD], src[:, 0:KD]).then_inc(wq_current, 1)
                pool.tensor_copy(wq_cur[:, parity, KD:2 * KD], src[:, 0:KD]).then_inc(wq_current, 1)
                pool.tensor_copy(wq_cur[:, parity, P:P + KD + 1], src).then_inc(wq_current, 1)

            def keys(g, parity, first=False):
                if not first:
                    pool.wait_ge(k_low, NQ)
                    pool.wait_ge(context_added, g * 8 - 8)
                    pool.sem_inc(pool_waited, 1)
                b = g // H
                pool.tensor_copy(k_hh_cur[:, parity, :], k_hh[:, bass.ds(b * S, S)]).then_inc(keys_current, 1)
                pool.tensor_copy(k_l1_cur[:, parity, :], k_l1[:, bass.ds(b * S, S)]).then_inc(keys_current, 1)
                pool.tensor_copy(ckv_cur[:, parity, :],
                                 ckv[:, bass.ds(b * KT, KT), :].rearrange("p t c -> p (t c)"))\
                    .then_inc(keys_current, 1)

            pool.wait_ge(wq_made, 1)
            query_weights(0, 0, True)
            query_weights(1, 1, True)
            pool.wait_ge(k_low, 2)
            pool.wait_ge(c_copied, 2)
            keys(0, 0, True)
            keys(1, 1, True)
            pool.wait_ge(k_low, NQ)
            pool.wait_ge(c_copied, NQ)
            query_weights(2, 0)

            def pair(j):
                new_batch = isinstance(j, int) and j % (H // 2) == 0
                query_weights(j * 2 + 1, 1)
                if new_batch:
                    keys(j * 2, 0)
                if not (isinstance(j, int) and j == PAIRS - 1):
                    query_weights(j * 2 + 2, 0)
                if new_batch:
                    keys(j * 2 + 1, 1)

            pool.wait_ge(routed, 1)
            pool.wait_ge(zeros_stored, 16)

            def dispatch(j, first=False):
                for t in range(DISPATCH):
                    for k in range(TOPK):
                        n = j * (DISPATCH * TOPK) + (t * TOPK + k)
                        if not (first and t == 0):
                            pool.wait_ge(routed, 1)
                            pool.wait_ge(rows_sent_k[k], (j * DISPATCH + t) * 16)
                        tt = bass.ds(j * DISPATCH + t, 1)
                        pool.tensor_copy(row_st[:, k, :], xn[:, tt, :].rearrange("p a d -> p (a d)"))\
                            .then_inc(staged, 1)
                        pool.tensor_copy(slot_st[:, k, :], slot_of[:, k, tt]).then_inc(staged, 1)
                        pool.wait_ge(staged, n * 2 + 2)
                        pool.sem_inc(pool_waited, 1)
                        pool.indirect_dma_start(
                            out=xs_dram, out_offset=bass.IndirectOffsetOnAxis(ap=slot_st[:, k, :], axis=0),
                            in_=row_st[:, k, :], in_offset=None).then_inc(rows_sent_k[k], 16)

            pair(1)
            dispatch(0, True)
            with pool.Fori(1, NT // DISPATCH - 1) as j:
                pair(j + 1)
                dispatch(j)
            pair(NT // DISPATCH)
            dispatch(NT // DISPATCH - 1)
            with pool.Fori(NT // DISPATCH + 1, SPLIT) as j:
                pair(j)
            pair(SPLIT)

            def store_tile(i, parity):
                pool.wait_ge(y_copied, i + 1)
                pool.dma_start(ys_dram[bass.ds(i * SLOTS, SLOTS), :].rearrange("(a p) d -> p a d", p=P),
                               y_out[:, parity, :, :]).then_inc(y_stored[parity], 16)

            over_tiles(pool, store_tile)
            pool.wait_ge(y_stored[0], (NTILES + 1) // 2 * 16)
            pool.wait_ge(y_stored[1], NTILES // 2 * 16)
            n_staged = NT * TOPK * 2

            def fetch(i):
                if not isinstance(i, int):
                    pool.wait_ge(routed, 1)
                    pool.wait_ge(rows_added, i)
                for t in range(COMBINE):
                    for k in range(TOPK):
                        at = t * TOPK + k
                        last = pool.tensor_copy(slot_st[:, at, :], slot_of[:, k, bass.ds(i * COMBINE + t, 1)])
                        last.then_inc(staged, 1)
                pool.wait_ge(y_stored[0], (NTILES + 1) // 2 * 16)
                pool.wait_ge(staged, i * (COMBINE * TOPK) + (n_staged + COMBINE * TOPK))
                pool.sem_inc(pool_waited, 1)
                for at in range(COMBINE * TOPK):
                    pool.indirect_dma_start(
                        out=fetched[:, at, :], out_offset=None, in_=ys_dram,
                        in_offset=bass.IndirectOffsetOnAxis(ap=slot_st[:, at, :], axis=0)).then_inc(rows_fetched, 16)

            fetch(0)
            new = list(range(SPLIT + 1, PAIRS - 1, H // 2))
            for at in new:
                pair(at)
                fetch(at - SPLIT)
                with pool.Fori(at + 1, min(at + H // 2, PAIRS - 1)) as j:
                    pair(j)
                    fetch(j - SPLIT)
            pair(PAIRS - 1)

        @block.scalar
        def _(act):
            act.wait_ge(var_ready, 1)
            act.activation(rstd[:, 0, :], rstd[:, 1, :], ACT.Sqrt).then_inc(std_ready, 1)
            act.wait_ge(d_w, 16 * NLOADS)
            act.wait_ge(consts_made, 3)
            with act.Fori(0, NQ // 2) as j:
                for par in range(2):
                    ck = j * 2 + par
                    here = bass.ds(ck * QC, QC)
                    act.wait_ge(xT_ready, ck + 1)
                    act.activation(xT_st[:, par, :], sc[0][:, 0:QC], ACT.Copy).then_inc(xT_copied, 1)
                    act.wait_ge(k_ready, ck + 1)
                    act.activation(k_hh[:, here], sc[1][:, 0:QC], ACT.Identity, bias=b_k[:, 0:1])\
                       .then_inc(k_copied, 1)
                    act.activation(k_h1[0:KD, here], sc[1][0:KD, 0:QC], ACT.Identity, bias=b_k[0:KD, 0:1])\
                       .then_inc(k_top, 1)
                    act.wait_ge(cq_ready, ck + 1)
                    act.activation(xq[:, here], mx[:, 0:QC], ACT.Identity, bias=b_cq[:, 0:1])\
                       .then_inc(cq_copied, 1)

            act.wait_ge(gap_ready, 1)
            act.activation(first_w[:, 1, :], first_w[:, 0, :], ACT.Exp).then_inc(gap_exp, 1)

            def gelus(i, parity):
                act.wait_ge(b_in[parity], (i // 2) * 16 + 16)
                if not (isinstance(i, int) and i < 2):
                    act.wait_ge(yT_ready, i - 1)
                for f in range(FT):
                    act.wait_ge(hidden_ready, i * FT + (f + 1))
                    act.activation(h_t[parity][:, f * SLOTS:(f + 1) * SLOTS], ps[:, f * 512:f * 512 + SLOTS],
                                   ACT.Gelu, bias=b12_t[:, parity, f:f + 1]).then_inc(hidden_done, 1)

            def experts():
                over_tiles(act, gelus)

            def q_high(n, c, parity):
                act.wait_ge(q_ready, n * 4 + (2 * c + 1))
                act.activation(q_hl[:, parity, c * QC:(c + 1) * QC], aux, ACT.Copy).then_inc(q_hi_done, 1)

            def q_one(n, c, parity):
                act.wait_ge(q_ready, n * 4 + (2 * c + 2))
                act.activation(q_h1[:, parity, c * QC:(c + 1) * QC], aux, ACT.Copy).then_inc(q_h1_done, 1)

            def context_out(g, c, first=False):
                act.wait_ge(context_added, g * 8 + (4 * c + 4))
                if not first:
                    act.wait_ge(head_out_ready, g * 4 + (2 * c - 2))
                act.activation(ctx_sb[:, c, :], cx, ACT.Copy).then_inc(context_copied, 1)

            def head(g, par, attend=True, ahead=2, first=False, second=False, late=None):
                for s in range(8):
                    if attend:
                        act.wait_ge(scores_ready, g * 8 + (s + 1))
                        if not (first and s < 4):
                            act.wait_ge(context_added, g * 8 + (s - 3))
                        act.activation(probs[:, s % 4, :], sc[s % 2], ACT.Exp, scale=SCALE)\
                            .then_inc(probs_ready, 1)
                    if s == 0 and attend and not first:
                        context_out(g - 1, 1, second)
                    if s == 4 and attend:
                        context_out(g, 0, first)
                    if s == 1 and ahead >= 1:
                        q_high(g + 1, 1, 1 - par)
                    if s == 2 and ahead >= 1:
                        q_one(g + 1, 1, 1 - par)
                    if s == 5 and ahead >= 2:
                        q_high(g + 2, 0, par)
                    if s == 6 and ahead >= 2:
                        q_one(g + 2, 0, par)

            q_high(0, 0, 0)
            q_one(0, 0, 0)
            head(-1, 1, attend=False)
            run_heads(act, head, experts)
            context_out(NHEADS - 1, 1)

        @block.vector
        def _(dve):
            steps = [0]

            def link(ins):
                steps[0] += 1
                ins.then_inc(dve_done, 1)
                dve.wait_ge(dve_done, steps[0])

            for i in range(4):
                dve.wait_ge(d_x[i], 16)
                for t in range(8 * i, 8 * i + 8):
                    last = dve.bn_stats(stat[:, t, :], acc[:, t, :])
            link(last)
            for t in range(NT):
                last = dve.bn_aggr(mv[:, t, :], stat[:, t, :])
            link(last)
            std, var, r, r3 = (rstd[:, i, :] for i in range(4))
            dve.tensor_scalar(var, mv[:, :, 1:2].rearrange("p t a -> p (t a)"), EPS, None, ALU.add)\
               .then_inc(var_ready, 1)
            dve.wait_ge(std_ready, 1)
            link(dve.reciprocal(r, std))
            link(dve.tensor_tensor(r3, r, r, ALU.mult))
            link(dve.tensor_tensor(r3, r3, var, ALU.mult))
            link(dve.tensor_scalar(r3, r3, -0.5, 1.5, ALU.mult, ALU.add))
            link(dve.tensor_tensor(r, r, r3, ALU.mult))
            dve.wait_ge(wT_ready, 1)
            dve.wait_ge(consts_made, 2)
            pq = sc[0][:, 0:H * 33].rearrange("p (h k) -> p h k", h=H)
            pk = sc[0][:, 512:512 + H * 33]
            pv = sc[1][:, 0:H * 33].rearrange("p (h k) -> p h k", h=H)
            q3 = uq3.rearrange("p (h k) -> p h k", h=H)
            v2 = uv2.rearrange("p (h k) -> p h k", h=H)
            for g in range(3):
                dve.tensor_copy(q3[:, :, g * DC:(g + 1) * DC], pq[:, :, 0:DC])
            dve.tensor_copy(q3[:, :, 96:97], pq[:, :, DC:DC + 1])
            dve.tensor_copy(q3[:, :, 97:98], pq[:, :, DC:DC + 1])
            dve.tensor_copy(ukT, pk)
            dve.tensor_copy(v2[:, :, 0:33], pv)
            link(dve.tensor_copy(v2[:, :, 64:97], pv))
            dve.tensor_copy(lo_mask, ident[:, 97:98]).then_inc(wT_copied, 1)
            dve.wait_ge(prod_ready, 2)
            dve.wait_ge(ident_made, 1)
            dve.wait_ge(d_w, 16 * NLOADS)
            f = fmat[:, 0:H * (KD + 1)].rearrange("p (h k) -> p h k", h=H)
            lo = uv2[:, 0:H * (KD + 1)]
            pa = sc[1][:, 512:512 + H * 33].rearrange("p (h k) -> p h k", h=H)
            dve.tensor_copy(f[:, :, 0:DC], pa[:, :, 0:DC])
            dve.tensor_copy(f[:, :, KD:KD + 1], pa[:, :, DC:DC + 1])
            dve.tensor_copy(hi_mask, ident[:, 96:97])
            link(dve.tensor_copy(f[:, :, DC:KD], qr98.rearrange("p (h k) -> p h k", h=H)))
            link(dve.memset(hi_mask[0:32], 1.0))
            link(dve.memset(hi_mask[64:96], 1.0))
            link(dve.memset(lo_mask[32:64], 1.0))
            ff = fmat[:, 0:H * (KD + 1)]
            wqf = wq_abs[:, :, :].rearrange("p h k -> p (h k)")
            link(dve.tensor_copy(wqf, ff))
            link(dve.tensor_tensor(lo, ff, wqf.bitcast(FP32), ALU.subtract))
            link(dve.tensor_scalar(ff, wqf.bitcast(FP32), hi_mask, None, ALU.mult))
            dve.scalar_tensor_tensor(wqf, lo, lo_mask, ff, ALU.mult, ALU.add).then_inc(wq_made, 1)
            dve.tensor_tensor(wvo[:, :, D:OW].rearrange("p h a -> p (h a)"), ident[:, 32:33].to_broadcast([P, H]),
                              ident[:, 96:97].to_broadcast([P, H]), ALU.add)
            dve.tensor_copy(wvo[:, :, 0:D], mx.rearrange("p (h d) -> p h d", h=H)).then_inc(wvo_made, 1)

            def normalise(ck, par, first=False):
                if not first:
                    dve.wait_ge(xT_ready, ck - 1)
                    dve.wait_ge(xn_kept, ck - 1)
                for t in range(4):
                    src = acc[:, bass.ds(ck * 4 + t, 1), :].rearrange("p a d -> p (a d)")
                    mean = mv[:, bass.ds(ck * 4 + t, 1), 0:1].rearrange("p a d -> p (a d)")
                    last = dve.tensor_scalar(xn_st[:, par, t, :], src, mean, r[:, bass.ds(ck * 4 + t, 1)],
                                             ALU.subtract, ALU.mult)
                last.then_inc(xn_ready, 1)

            def low_parts(ck):
                here = bass.ds(ck * QC, QC)
                dve.wait_ge(k_top, ck + 1)
                dve.scalar_tensor_tensor(k_l1[0:KD, here], sc[1][0:KD, 0:QC], b_k[0:KD, 0:1],
                                         k_hh[0:KD, here].bitcast(FP32), ALU.add, ALU.subtract)\
                    .then_inc(k_low, 1)
                dve.wait_ge(cq_copied, ck + 1)
                dve.scalar_tensor_tensor(xq[64:96, here], mx[64:96, 0:QC], b_cq[64:96, 0:1],
                                         xq[64:96, here].bitcast(FP32), ALU.add, ALU.subtract)\
                    .then_inc(cq_low, 1)
                dve.wait_ge(cg_ready, ck + 1)
                cg = mx[:, 512:512 + 4 * 64].rearrange("p (t k) -> p t k", t=4)
                dve.tensor_copy(logits[:, bass.ds(ck * 4, 4), :], cg[:, :, DC:DC + H])
                dve.tensor_tensor(ckv[:, bass.ds(ck * 4, 4), 0:DC], cg[:, :, 0:DC],
                                  bkv_bc[:, :].unsqueeze(1).to_broadcast([P, 4, DC]), ALU.add).then_inc(c_copied, 1)

            dve.wait_ge(consts_made, 3)
            normalise(0, 0, True)
            normalise(1, 1, True)
            low_parts(0)
            with dve.Fori(1, NQ // 2) as j:
                normalise(j * 2, 0)
                low_parts(j * 2 - 1)
                normalise(j * 2 + 1, 1)
                low_parts(j * 2)
            low_parts(NQ - 1)
            dve.wait_ge(bo_added, NQ)

            dve.wait_ge(consts_made, 5)
            dve.wait_ge(c_copied, NQ)
            TE = NT * E
            big = 1.7e38

            def rt(i, n=TE):
                return prep[:, i // 4, (i % 4) * TE:(i % 4) * TE + n]

            def te(v):
                return v.rearrange("p (t e) -> p t e", e=E)

            def over_e(v):
                return v.unsqueeze(2).to_broadcast([P, NT, E])
            one_hot = [rt(0), rt(1)]
            work, rest, both, pre, tot_a, tot_b = (rt(i) for i in range(2, 8))
            small = rt(8)
            best = [small[:, 0:NT], small[:, NT:2 * NT]]
            pick = small[:, 2 * NT:3 * NT]
            fall = falling[:, :].unsqueeze(1).to_broadcast([P, NT, E])
            src = logits[:, :, :]
            for k in range(TOPK):
                link(dve.reduce_max(best[k], src, AX.X))
                link(dve.tensor_tensor(te(work), src, over_e(best[k]), ALU.is_equal))
                link(dve.tensor_tensor(te(work), te(work), fall, ALU.mult))
                link(dve.reduce_max(pick, te(work), AX.X))
                link(dve.tensor_tensor(te(one_hot[k]), fall, over_e(pick), ALU.is_equal))
                if k == 0:
                    link(dve.tensor_scalar(work, one_hot[0], -2 * big, big, ALU.mult, ALU.add))
                    link(dve.tensor_tensor(te(rest), src, te(work), ALU.min))
                    src = te(rest)
            dve.tensor_tensor(both, one_hot[0], one_hot[1], ALU.add).then_inc(chosen, 1)
            dve.tensor_tensor(first_w[:, 0, :], best[1], best[0], ALU.subtract).then_inc(gap_ready, 1)
            dve.wait_ge(gap_exp, 1)
            link(dve.tensor_scalar(best[0], first_w[:, 1, :], 1.0, None, ALU.add))
            link(dve.reciprocal(first_w[:, 0, :], best[0]))
            link(dve.tensor_tensor(first_w[:, 1, :], first_w[:, 1, :], first_w[:, 0, :], ALU.mult))
            dve.wait_ge(counted, 1)
            link(dve.tensor_copy(pre, mx[:, 0:TE]))
            link(dve.tensor_copy(tot_a, mx[:, 512:512 + TE]))
            link(dve.tensor_tensor(pre, pre, tot_a, ALU.subtract))
            src, dst = tot_a, tot_b
            for step in (1, 2, 4, 8, 16):
                link(dve.tensor_copy(dst[:, 0:step * E], src[:, 0:step * E]))
                link(dve.tensor_tensor(dst[:, step * E:], src[:, step * E:], src[:, 0:TE - step * E], ALU.add))
                src, dst = dst, src
            link(dve.tensor_tensor(pre, pre, src, ALU.add))
            tiles_i = rt(9, E).bitcast(I32)
            cum = [rt(10, E), rt(11, E)]
            link(dve.tensor_scalar(cum[0], src[:, TE - E:TE], float(SLOTS - 1), None, ALU.add))
            link(dve.tensor_copy(tiles_i, cum[0]))
            link(dve.tensor_scalar(tiles_i, tiles_i, SLOTS.bit_length() - 1, None, ALU.arith_shift_right))
            link(dve.tensor_copy(cum[0], tiles_i))
            link(dve.tensor_copy(rest[:, 0:E], cum[0]))
            a, b_ = cum
            for step in (1, 2, 4):
                link(dve.tensor_copy(b_[:, 0:step], a[:, 0:step]))
                link(dve.tensor_tensor(b_[:, step:], a[:, step:], a[:, 0:E - step], ALU.add))
                a, b_ = b_, a
            cmp_ = fetched[:, 0:3, :].rearrange("p a d -> p (a d)")[:, 0:NTILES * E].rearrange("p (t e) -> p t e", e=E)
            link(dve.tensor_tensor(cmp_, tile_no[:, :].unsqueeze(2).to_broadcast([P, NTILES, E]),
                                   a.unsqueeze(1).to_broadcast([P, NTILES, E]), ALU.is_ge))
            link(dve.reduce_sum(work[:, 0:NTILES], cmp_, AX.X))
            link(dve.tensor_scalar(expert_of[:, :], work[:, 0:NTILES], float(E - 1), None, ALU.min))
            link(dve.tensor_tensor(rest[:, 0:E], a, rest[:, 0:E], ALU.subtract))
            link(dve.tensor_scalar(rest[:, 0:E], rest[:, 0:E], float(SLOTS), None, ALU.mult))
            link(dve.tensor_tensor(te(pre), te(pre), rest[:, 0:E].unsqueeze(1).to_broadcast([P, NT, E]), ALU.add))
            for k in range(TOPK):
                link(dve.tensor_tensor(work, one_hot[k], pre, ALU.mult))
                link(dve.reduce_sum(pick, te(work), AX.X))
                last = dve.tensor_copy(slot_of[:, k, :], pick)
                if k == 0:
                    link(last)
            last.then_inc(routed, 1)

            def slots_transposed(i, parity):
                dve.wait_ge(xgT_ready, i + 1)
                dve.tensor_copy(xgT[:, parity, :], mx[:, 0:SLOTS]).then_inc(xgT_copied, 1)

            def outputs(i, parity):
                dve.wait_ge(yT_ready, i + 1)
                if not (isinstance(i, int) and i == 0):
                    dve.wait_ge(y_ready, i)
                dve.tensor_scalar(yT, mx[:, 512:512 + SLOTS], b12_t[:, parity, FT:FT + 1], None, ALU.add)\
                    .then_inc(yT_copied, 1)
                dve.wait_ge(y_ready, i + 1)
                if not (isinstance(i, int) and i < 2):
                    dve.wait_ge(y_stored[parity], (i // 2) * 16)
                dve.tensor_copy(y_out[:, parity, :, :].rearrange("p a d -> p (a d)"), aux[:, 0:SLOTS])\
                    .then_inc(y_copied, 1)

            def experts():
                def tile(i, parity):
                    if not (isinstance(i, int) and i == NTILES - 1):
                        slots_transposed(i + 1, 1 - parity)
                    outputs(i, parity)
                slots_transposed(0, 0)
                over_tiles(dve, tile)

            def add_experts(i):
                dve.wait_ge(rows_fetched, i * (16 * COMBINE * TOPK) + 16 * COMBINE * TOPK)
                for k in range(TOPK):
                    if k:
                        dve.wait_ge(half_added, i + 1)
                    for t in range(COMBINE):
                        tt = bass.ds(i * COMBINE + t, 1)
                        a = acc[:, tt, :].rearrange("p a d -> p (a d)")
                        last = dve.scalar_tensor_tensor(a, fetched[:, t * TOPK + k, :], first_w[:, k, tt], a,
                                                        ALU.mult, ALU.add)
                    last.then_inc(rows_added if k else half_added, 1)

            def q_low(n, c, parity):
                dve.wait_ge(q_hi_done, n * 2 + (c + 1))
                lo_part = q_hl[KD:P, parity, c * QC:(c + 1) * QC]
                dve.tensor_tensor(lo_part, aux[KD:P, :], lo_part.bitcast(FP32), ALU.subtract)\
                    .then_inc(q_lo_done, 1)

            def add_out(g, c, half):
                dve.wait_ge(head_out_ready, g * 4 + (2 * c + half + 1))
                o = aux[:, 0:2 * OW].rearrange("p (t k) -> p t k", t=2)
                dve.reciprocal(rsum[:, half, :], o[:, :, D:OW].rearrange("p t a -> p (t a)")).then_inc(recip_done, 1)
                dve.wait_ge(recip_done, g * 4 + (2 * c + half + 1))
                b = g // H
                for t in range(2):
                    a = acc[:, bass.ds(b * KT + (c * 4 + half * 2 + t), 1), :].rearrange("p a d -> p (a d)")
                    last = dve.scalar_tensor_tensor(a, o[:, t, 0:D], rsum[:, half, t:t + 1], a, ALU.mult, ALU.add)
                last.then_inc(head_out_added, 1)

            def max_rows(n, c, first=False):
                dve.wait_ge(maxT_ready, n * 2 + (c + 1))
                if not first:
                    dve.wait_ge(mrow_moved[c], n * 16)
                dve.tensor_scalar(mrow[:, c, :], mx[0:4, 0:P], -1.0, None, ALU.mult).then_inc(mrow_ready, 1)

            def head(g, par, attend=True, ahead=2, first=False, second=False, late=None):
                for s in range(8):
                    if s == 0 and attend:
                        max_rows(g, 1, first)
                    if s == 4 and ahead >= 1:
                        max_rows(g + 1, 0, not attend)
                    if attend and not first:
                        if s == 0:
                            add_out(g - 1, 0, 1)
                        if s in (3, 4):
                            add_out(g - 1, 1, s - 3)
                    if s == 1 and ahead >= 1:
                        q_low(g + 1, 1, 1 - par)
                    if s == 5 and ahead >= 2:
                        q_low(g + 2, 0, par)
                    if s == 7 and attend:
                        add_out(g, 0, 0)
                    if s == 6 and par == 1 and late is not None:
                        add_experts(late)
                    if ahead >= 1:
                        dve.wait_ge(max_ready, g * 8 + (9 + s))
                        dve.reduce_max(mcol[:, 1 - par, s:s + 1], mx, AX.X).then_inc(max_done, 1)

            q_low(0, 0, 0)
            head(-1, 1, attend=False)
            run_heads(dve, head, experts)
            add_out(NHEADS - 1, 0, 1)
            add_out(NHEADS - 1, 1, 0)
            add_out(NHEADS - 1, 1, 1)

        @block.tensor
        def _(pe):
            pe.wait_ge(d_w, 16 * NLOADS)
            pe.wait_ge(ident_made, 1)
            for w, dst in ((uq33, sc[0][:, 0:264]), (uk33, sc[0][:, 512:776]), (uv33, sc[1][:, 0:264])):
                for h in range(H):
                    last = pe.transpose(dst[:, h * 33:(h + 1) * 33], w[:, h * DK:(h + 1) * DK], ident[0:33, 0:33])
            last.then_inc(wT_ready, 1)
            pe.wait_ge(wT_copied, 1)
            for h in range(H):
                last = pe.matmul(sc[1][:, 512 + h * 33:512 + (h + 1) * 33], uq3[:, h * P:(h + 1) * P],
                                 ukT[:, h * 33:(h + 1) * 33], start=True, stop=True)
            last.then_inc(prod_ready, 1)
            for h in range(H):
                last = pe.matmul(mx[:, h * D:(h + 1) * D], uv2[:, h * P:(h + 1) * P],
                                 wo_sb[:, h, :], start=True, stop=True)
            last.then_inc(prod_ready, 1)
            pe.wait_ge(wvo_made, 1)
            pe.wait_ge(wq_made, 1)

            def latents(ck, par, first=False):
                pe.wait_ge(xn_ready, ck + 1)
                for t in range(4):
                    last = pe.transpose(sc[0][:, t * P:(t + 1) * P], xn_st[:, par, t, :], ident[:, :])
                last.then_inc(xT_ready, 1)
                pe.wait_ge(xT_copied, ck + 1)
                if not first:
                    pe.wait_ge(k_low, ck)
                    pe.wait_ge(k_top, ck)
                pe.matmul(sc[1][:, 0:QC], w_k2[:, :], xT_st[:, par, :], start=True, stop=True).then_inc(k_ready, 1)
                if not first:
                    pe.wait_ge(cq_low, ck)
                pe.matmul(mx[:, 0:QC], w_cq[:, :], xT_st[:, par, :], start=True, stop=True).then_inc(cq_ready, 1)
                if not first:
                    pe.wait_ge(c_copied, ck)
                for t in range(4):
                    last = pe.matmul(mx[:, 512 + t * 64:512 + t * 64 + DC + H], xT_st[:, par, t * P:(t + 1) * P],
                                     w_cg[:, :], start=True, stop=True)
                last.then_inc(cg_ready, 1)

            latents(0, 0, True)
            latents(1, 1)
            with pe.Fori(1, NQ // 2) as j:
                latents(j * 2, 0)
                latents(j * 2 + 1, 1)
            pe.wait_ge(k_top, NQ)
            pe.wait_ge(k_low, NQ)
            pe.wait_ge(cq_low, NQ)
            pe.wait_ge(c_copied, NQ)
            pe.wait_ge(chosen, 1)
            pe.matmul(mx[:, 0:NT * E], upper[:, :], prep[:, 1, 0:NT * E], start=True, stop=True)
            pe.matmul(mx[:, 512:512 + NT * E], ones[:, :], prep[:, 1, 0:NT * E], start=True, stop=True)\
                .then_inc(counted, 1)

            def query(n, c, form, parity):
                pe.wait_ge(wq_current, n * 3 + 3)
                pe.matmul(aux, wq_cur[:, parity, form * P:(form + 1) * P],
                          xq[:, bass.ds((n // H) * S + c * QC, QC)], start=True, stop=True).then_inc(q_ready, 1)

            def head_out(g, c, half):
                h = g % H
                pe.wait_ge(context_copied, g * 2 + (c + 1))
                for t in range(2):
                    i = half * 2 + t
                    last = pe.matmul(aux[:, t * OW:(t + 1) * OW], ctx_sb[:, c, i * P:(i + 1) * P],
                                     wvo[:, bass.ds(h, 1), :].rearrange("p a k -> p (a k)"), start=True, stop=True)
                last.then_inc(head_out_ready, 1)

            def fill(g, s, par, attend, ahead, first):
                before = attend and not first
                if s == 0 and before:
                    pe.wait_ge(head_out_added, g * 4 - 3)
                    head_out(g - 1, 0, 1)
                if s == 1 and ahead >= 1:
                    if before:
                        pe.wait_ge(head_out_added, g * 4 - 2)
                    else:
                        pe.wait_ge(q_h1_done, g * 2 + 3)
                    query(g + 1, 1, 0, 1 - par)
                if s == 2 and ahead >= 1:
                    pe.wait_ge(q_lo_done, g * 2 + 4)
                    query(g + 1, 1, 1, 1 - par)
                if s == 3 and before:
                    if ahead >= 1:
                        pe.wait_ge(q_h1_done, g * 2 + 4)
                    else:
                        pe.wait_ge(head_out_added, g * 4 - 2)
                    head_out(g - 1, 1, 0)
                if s == 4 and before:
                    pe.wait_ge(head_out_added, g * 4 - 1)
                    head_out(g - 1, 1, 1)
                if s == 5 and ahead >= 2:
                    if before:
                        pe.wait_ge(head_out_added, g * 4)
                    else:
                        pe.wait_ge(q_h1_done, g * 2 + 4)
                    query(g + 2, 0, 0, par)
                if s == 6 and ahead >= 2:
                    pe.wait_ge(q_lo_done, g * 2 + 5)
                    query(g + 2, 0, 1, par)
                if s == 7 and attend:
                    if ahead >= 2:
                        pe.wait_ge(q_h1_done, g * 2 + 5)
                    else:
                        pe.wait_ge(head_out_added, g * 4)
                    head_out(g, 0, 0)

            def add_context(g, s, par, first_unit=False):
                c, p = s // 4, s % 4
                pe.wait_ge(probs_ready, g * 8 + (s + 1))
                if p == 0 and not first_unit:
                    pe.wait_ge(context_copied, g * 2 + c)
                for i in range(2):
                    kt = 2 * p + i
                    last = pe.matmul(cx[CW * i:CW * (i + 1), :], ckv_cur[:, par, kt * CW:(kt + 1) * CW],
                                     probs[:, s % 4, i * QC:(i + 1) * QC], start=(p == 0), stop=(p == 3))
                last.then_inc(context_added, 1)

            def head(g, par, attend=True, ahead=2, first=False, second=False, late=None):
                for s in range(8):
                    c, p = s // 4, s % 4
                    if attend:
                        if s == 0:
                            pe.wait_ge(keys_current, (g // H) * 6 + (3 * par + 3))
                        if p == 0:
                            pe.wait_ge(q_lo_done, g * 2 + (c + 1))
                            pe.wait_ge(mrow_moved[c], g * 16 + 16)
                        if not (first and s < 2):
                            pe.wait_ge(probs_ready, g * 8 + (s - 1))
                        for i in range(2):
                            kt = 2 * p + i
                            o = sc[s % 2][:, i * QC:(i + 1) * QC]
                            pe.matmul(o, k_hh_cur[:, par, kt * P:(kt + 1) * P], q_hl[:, par, c * QC:(c + 1) * QC],
                                      start=True, stop=False)
                            last = pe.matmul(o, k_l1_cur[:, par, kt * P:(kt + 1) * P],
                                             q_h1[:, par, c * QC:(c + 1) * QC], start=False, stop=True)
                        last.then_inc(scores_ready, 1)
                    fill(g, s, par, attend, ahead, first)
                    if s == 0 and attend:
                        transpose_max(g, 1, par)
                    if s == 4 and ahead >= 1:
                        transpose_max(g + 1, 0, 1 - par)
                    if attend:
                        if s > 0:
                            add_context(g, s - 1, par, first and s == 1)
                        elif not first:
                            add_context(g - 1, 7, 1 - par)
                    if ahead >= 1:
                        if s in (0, 4):
                            pe.wait_ge(q_h1_done, g * 2 + (3 + s // 4))
                            if attend or s == 4:
                                pe.wait_ge(mrow_ready, g * 2 + (2 + s // 4))
                        else:
                            pe.wait_ge(max_done, g * 8 + (8 + s))
                        for i in range(2):
                            last = pe.matmul(mx[:, i * QC:(i + 1) * QC], q_h1[:, 1 - par, s * P:(s + 1) * P],
                                             k_h1[:, bass.ds(((g + 1) // H) * S + i * QC, QC)],
                                             start=True, stop=True)
                        last.then_inc(max_ready, 1)

            def transpose_max(n, c, parity):
                pe.wait_ge(max_done, n * 8 + (4 * c + 4))
                pe.transpose(mx[0:4, 0:P], mcol[:, parity, 4 * c:4 * c + 4], ident[:, :]).then_inc(maxT_ready, 1)

            def slots_in(i, parity):
                pe.wait_ge(x_in[parity], (i // 2) * 16 + 16)
                if not (isinstance(i, int) and i == 0):
                    pe.wait_ge(xgT_copied, i)
                for a in range(2):
                    last = pe.transpose(mx[:, a * P:(a + 1) * P], xg[:, parity, a, :], ident[:, :])
                last.then_inc(xgT_ready, 1)

            def hidden(i, parity):
                pe.wait_ge(w1_in[parity], (i // 2) * 16 + 16)
                pe.wait_ge(xgT_copied, i + 1)
                for f in range(FT):
                    pe.matmul(ps[:, f * 512:f * 512 + SLOTS], w1_t[:, parity, f * P:(f + 1) * P],
                              xgT[:, parity, :], start=True, stop=True).then_inc(hidden_ready, 1)

            def output(i, parity):
                pe.wait_ge(w2_in[parity], (i // 2) * 16 + 16)
                if not (isinstance(i, int) and i == 0):
                    pe.wait_ge(yT_copied, i)
                for f in range(FT):
                    pe.wait_ge(hidden_done, i * FT + (f + 1))
                    last = pe.matmul(mx[:, 512:512 + SLOTS], w2_t[:, parity, f * P:(f + 1) * P],
                                     h_t[parity][:, f * SLOTS:(f + 1) * SLOTS], start=(f == 0), stop=(f == FT - 1))
                last.then_inc(yT_ready, 1)

            def slots_out(i, parity):
                pe.wait_ge(yT_copied, i + 1)
                if not (isinstance(i, int) and i == 0):
                    pe.wait_ge(y_copied, i)
                for a in range(2):
                    last = pe.transpose(aux[:, a * P:(a + 1) * P], yT[:, a * P:(a + 1) * P], ident[:, :])
                last.then_inc(y_ready, 1)

            def experts():
                pe.wait_ge(probs_ready, SPLIT * 16)
                pe.wait_ge(max_done, SPLIT * 16 + 8)
                pe.wait_ge(head_out_added, SPLIT * 8 - 3)

                def tile(i, parity):
                    last = isinstance(i, int) and i == NTILES - 1
                    if not last:
                        slots_in(i + 1, 1 - parity)
                    output(i, parity)
                    if not last:
                        hidden(i + 1, 1 - parity)
                    slots_out(i, parity)
                slots_in(0, 0)
                hidden(0, 0)
                over_tiles(pe, tile)
                pe.wait_ge(y_copied, NTILES)

            query(0, 0, 0, 0)
            pe.wait_ge(q_lo_done, 1)
            query(0, 0, 1, 0)
            pe.wait_ge(routed, 1)
            head(-1, 1, attend=False)
            run_heads(pe, head, experts)
            last_head = NHEADS - 1
            add_context(last_head, 7, 1)
            pe.wait_ge(head_out_added, 4 * last_head + 1)
            head_out(last_head, 0, 1)
            pe.wait_ge(head_out_added, 4 * last_head + 2)
            head_out(last_head, 1, 0)
            pe.wait_ge(head_out_added, 4 * last_head + 3)
            head_out(last_head, 1, 1)


_NAMES = ['L0_attn_h_t', 'L0_attn_W_DQ', 'L0_attn_b_DQ', 'L0_attn_W_UQ', 'L0_attn_b_UQ', 'L0_attn_W_DKV',
          'L0_attn_b_DKV', 'L0_attn_W_UK', 'L0_attn_b_UK', 'L0_attn_W_UV', 'L0_attn_b_UV', 'L0_attn_W_QR',
          'L0_attn_b_QR', 'L0_attn_W_KR', 'L0_attn_b_KR', 'L0_attn_W_O', 'L0_attn_b_O', 'L0_ffn_gate_w',
          'L0_ffn_w1', 'L0_ffn_w2']


def layout(inputs):
    import numpy as np
    arrays = {name: np.ascontiguousarray(inputs[name]) for name in _NAMES}
    b1 = inputs['L0_ffn_b1'].reshape(E, FT, P).transpose(0, 2, 1)
    arrays['b12'] = np.ascontiguousarray(np.concatenate([b1, inputs['L0_ffn_b2'].reshape(E, P, 1)], axis=2))
    return arrays


def kernel(**inputs):
    import concourse.bacc as bacc
    from concourse.bass_utils import run_bass_kernel_spmd

    nc = bacc.Bacc("TRN2", target_bir_lowering=False, num_devices=1)
    arrays = layout(inputs)
    args = [nc.dram_tensor(name, a.shape, mybir.dt.from_np(a.dtype), kind="ExternalInput").ap()
            for name, a in arrays.items()]
    args.append(nc.dram_tensor("out", (B, S, D), FP32, kind="ExternalOutput").ap())
    moe_transformer_layer(nc, *args)
    r = run_bass_kernel_spmd(nc, [arrays], core_ids=[0])
    return r.results[0]["out"]
```

```python
import concourse.bass as bass
from concourse import mybir
from contextlib import ExitStack

FP32 = mybir.dt.float32
FP32R = mybir.dt.float32r
U32 = mybir.dt.uint32
I32 = mybir.dt.int32
ALU = mybir.AluOpType
ACT = mybir.ActivationFunctionType
AX = mybir.AxisListType

P = 128
B, S, D = 4, 1024, 128
H, DK, DC, DR = 8, 128, 32, 32
NT = B * S // P
QC = 512
NC = S // QC
KT = S // P
NQ = B * S // QC
SCALE = 1.0 / (DK + DR) ** 0.5
EPS = 1e-5
KD = DC + DR
ROW_QB = KD
ROW_MAX = KD + 1
CW = 64
ONE = DC
OW = D + 1
NHEADS = B * H
F, E, TOPK = 512, 8, 2
FT = F // P
NTOK = B * S
SLOTS = 256
NTILES = (NTOK * TOPK + E * (SLOTS - 1)) // SLOTS
PAIRS = NHEADS // 2
SPLIT = 7
DISPATCH = 8
COMBINE = NT // (PAIRS - SPLIT - 1)


W_COLS = {"ident": P, "w_k2": P, "w_cq": P, "w_cg": DC + H, "w_qr": H * DR, "bkv": DC,
          "b_k": 1, "b_cq": 1, "hi_rows": 1, "lo_rows": 1, "sum_rows": 1}
C_COLS = {"bo": D, "upper": P, "ones": P, "falling": E, "tile_no": NTILES}


def columns(packed, widths):
    parts, at = {}, 0
    for name, width in widths.items():
        parts[name] = packed[:, at:at + width]
        at += width
    return parts


def moe_transformer_layer(nc, x, up, weights, wo, consts, w1, w2, b12, out):
    with ExitStack() as ctx:
        def sb(name, shape, dt=FP32):
            return ctx.enter_context(nc.sbuf_tensor(name, shape, dt))

        def sem(name):
            return ctx.enter_context(nc.semaphore(name))

        xn = sb("xn", [P, NT, D])
        acc = sb("acc", [P, NT, D])
        xT_st = sb("xT_st", [P, 2, QC])
        xq = sb("xq", [P, B * S], FP32R)
        k_hh = sb("k_hh", [P, B * S], FP32R)
        k_h1 = sb("k_h1", [P, B * S], FP32R)
        k_l1 = sb("k_l1", [P, B * S], FP32R)
        ckv = sb("ckv", [P, NT, CW])
        logits = sb("logits", [P, NT, H])
        wq_abs = sb("wq_abs", [P, H, KD + 1], FP32R)
        wvo = sb("wvo", [P, H, OW])
        packed_w = sb("packed_w", [P, sum(W_COLS.values())])
        packed_c = sb("packed_c", [P, sum(C_COLS.values())])
        W, C = columns(packed_w, W_COLS), columns(packed_c, C_COLS)
        ident, w_k2, w_cq, w_cg, b_k, b_cq = (W[n] for n in ("ident", "w_k2", "w_cq", "w_cg", "b_k", "b_cq"))
        wq_cur = sb("wq_cur", [P, 2, 2 * P], FP32R)
        k_hh_cur = sb("k_hh_cur", [P, 2, S], FP32R)
        k_l1_cur = sb("k_l1_cur", [P, 2, S], FP32R)
        ckv_cur = sb("ckv_cur", [P, 2, KT * CW])
        q_hl = sb("q_hl", [P, 2, S], FP32R)
        q_h1 = sb("q_h1", [P, 2, S], FP32R)
        mcol = sb("mcol", [P, 2, KT])
        mrow = sb("mrow", [4, 2, P], FP32R)
        ctx_sb = sb("ctx_sb", [P, 2, QC])
        rsum = sb("rsum", [P, 2, 2])
        probs = sb("probs", [P, 4, 2 * QC])
        stat = sb("stat", [P, NT, 6])
        mv = sb("mv", [P, NT, 2])
        rstd = sb("rstd", [P, 4, NT])

        first_w = sb("first_w", [P, 2, NT])
        slot_of = sb("slot_of", [P, 2, NT], U32)
        expert_of = sb("expert_of", [P, NTILES], U32)
        slot_st = sb("slot_st", [P, 2 * COMBINE, 1], U32)
        row_st = sb("row_st", [P, 2, D])
        fetched = sb("fetched", [P, 2 * COMBINE, D])

        xs_dram = nc.dram_tensor("x_sorted", (NTILES * SLOTS, D), FP32).ap()
        ys_dram = nc.dram_tensor("y_sorted", (NTILES * SLOTS, D), FP32).ap()

        ps = ctx.enter_context(nc.psum_tensor("ps", [P, 8 * 512], FP32))
        sc = [ps[:, 1024 * i:1024 * (i + 1)] for i in range(2)]
        mx = ps[:, 2048:3072]
        cx = ps[:, 3072:3584]
        aux = ps[:, 3584:4096]

        up33 = probs[0:DC + 1, 0:3, :]
        wo_sb = sb("wo_sb", [P, H, D])
        prep = sb("prep", [P, 3, H * P])
        uq3, uv2, fmat = prep[:, 0, :], prep[:, 1, :], prep[:, 2, :]
        w1_t = prep[:, 0:1, :].rearrange("p a (b f) -> p (a b) f", b=2)
        w2_t = prep[:, 1:2, :].rearrange("p a (b f) -> p (a b) f", b=2)
        h_t = [prep[:, 2, :], wo_sb[:, :, :].rearrange("p h d -> p (h d)")]
        xg = sb("xg", [P, 2, 2, D])
        y_out = sb("y_out", [P, 2, 2, D])
        xgT = xT_st[:, :, 0:SLOTS]
        yT = xT_st[:, 0, SLOTS:2 * SLOTS]
        b12_t = sb("b12_t", [P, 2, FT + 1])
        ukT = ctx_sb[:, 0, 0:H * 33]

        x_loaded = [sem(f"x_loaded{i}") for i in range(B)]
        up_loaded = sem("up_loaded")
        weights_loaded = sem("weights_loaded")
        wo_loaded = sem("wo_loaded")
        consts_loaded = sem("consts_loaded")
        prep_zeroed = sem("prep_zeroed")
        ones_set = sem("ones_set")
        zeros_made = sem("zeros_made")
        pool_done = sem("pool_done")
        dve_done = sem("dve_done")
        var_ready = sem("var_ready")
        std_ready = sem("std_ready")
        xn_ready = sem("xn_ready")
        wT_ready = sem("wT_ready")
        q3_made = sem("q3_made")
        kv_made = sem("kv_made")
        prod_ready = sem("prod_ready")
        wq_made = sem("wq_made")
        wvo_made = sem("wvo_made")
        xT_ready = sem("xT_ready")
        xT_copied = sem("xT_copied")
        k_ready = sem("k_ready")
        cq_ready = sem("cq_ready")
        cg_ready = sem("cg_ready")
        k_copied = sem("k_copied")
        k_low = sem("k_low")
        cq_copied = sem("cq_copied")
        cq_low = sem("cq_low")
        c_copied = sem("c_copied")
        k_top = sem("k_top")
        bo_added = sem("bo_added")
        counts_taken = sem("counts_taken")
        zeros_stored = sem("zeros_stored")
        gap_ready = sem("gap_ready")
        gap_exp = sem("gap_exp")
        chosen = sem("chosen")
        counted = sem("counted")
        routed = sem("routed")
        staged = sem("staged")
        pool_waited = sem("pool_waited")
        rows_sent_k = [sem(f"rows_sent{k}") for k in range(TOPK)]
        rows_fetched = sem("rows_fetched")
        rows_added = sem("rows_added")
        half_added = sem("half_added")
        x_in = [sem(f"slots_loaded{i}") for i in range(2)]
        w1_in = [sem(f"w1_loaded{i}") for i in range(2)]
        w2_in = [sem(f"w2_loaded{i}") for i in range(2)]
        b_in = [sem(f"expert_biases_loaded{i}") for i in range(2)]
        xgT_ready = sem("xgT_ready")
        xgT_copied = sem("xgT_copied")
        hidden_ready = sem("hidden_ready")
        hidden_done = sem("hidden_done")
        yT_ready = sem("yT_ready")
        yT_copied = sem("yT_copied")
        y_ready = sem("y_ready")
        y_copied = sem("y_copied")
        y_stored = [sem(f"y_stored{i}") for i in range(2)]
        scores_ready = sem("scores_ready")
        probs_ready = sem("probs_ready")
        context_added = sem("context_added")
        context_copied = sem("context_copied")
        max_ready = sem("max_ready")
        max_done = sem("max_done")
        maxT_ready = sem("maxT_ready")
        mrow_ready = sem("mrow_ready")
        mrow_moved = [sem(f"mrow_moved{c}") for c in range(2)]
        q_ready = sem("q_ready")
        q_hi_done = sem("q_hi_done")
        q_lo_done = sem("q_lo_done")
        q_h1_done = sem("q_h1_done")
        head_out_ready = sem("head_out_ready")
        recip_done = sem("recip_done")
        head_out_added = sem("head_out_added")
        keys_current = sem("keys_current")
        wq_current = sem("wq_current")
        out_stored = sem("out_stored")

        block = ctx.enter_context(nc.Block())

        xv = x.rearrange("b (t p) d -> p (b t) d", p=P)
        ov = out.rearrange("b (t p) d -> p (b t) d", p=P)

        def run_heads(eng, head, experts):
            head(0, 0, first=True)
            head(1, 1, second=True)
            with eng.Fori(1, SPLIT) as j:
                head(j * 2, 0)
                head(j * 2 + 1, 1)
            experts()
            with eng.Fori(SPLIT, PAIRS - 1) as j:
                head(j * 2, 0, late=j - SPLIT)
                head(j * 2 + 1, 1, late=j - SPLIT)
            head(NHEADS - 2, 0, ahead=1)
            head(NHEADS - 1, 1, ahead=0)

        def over_tiles(eng, tile):
            tile(0, 0)
            tile(1, 1)
            with eng.Fori(1, NTILES // 2) as j:
                tile(j * 2, 0)
                tile(j * 2 + 1, 1)
            tile(NTILES - 1, 0)

        @block.sync
        def _(sp):
            def load_x(b):
                here = slice(b * KT, (b + 1) * KT)
                sp.dma_start(acc[:, here, :], xv[:, here, :]).then_inc(x_loaded[b], 16)
            load_x(0)
            sp.dma_start(up33, up).then_inc(up_loaded, 16)
            sp.dma_start(packed_w[:, :], weights).then_inc(weights_loaded, 16)
            load_x(1)
            sp.dma_start(wo_sb[:, :, :], wo.rearrange("(h k) d -> k h d", k=DK)).then_inc(wo_loaded, 16)
            load_x(2)
            load_x(3)
            sp.dma_start(packed_c[:, :], consts).then_inc(consts_loaded, 16)

            def move_max(n, c, parity):
                sp.wait_ge(mrow_ready, n * 2 + (c + 1))
                sp.dma_start(q_h1[ROW_MAX:ROW_MAX + 1, parity, c * QC:(c + 1) * QC].bitcast(FP32),
                             mrow[:, c, :].bitcast(FP32)).then_inc(mrow_moved[c], 16)

            def load_tile(i, parity):
                first = isinstance(i, int) and i < 2
                e = sp.value_load(expert_of[0:1, bass.ds(i, 1)], min_val=0, max_val=E - 1)
                if not first:
                    sp.wait_ge(xgT_ready, i - 1)
                sp.dma_start(xg[:, parity, :, :],
                             xs_dram[bass.ds(i * SLOTS, SLOTS), :].rearrange("(a p) d -> p a d", p=P))\
                    .then_inc(x_in[parity], 16)
                if not first:
                    sp.wait_ge(hidden_ready, i * FT - FT)
                sp.dma_start(w1_t[:, parity, :], w1[bass.ds(e, 1), :, :].rearrange("a d f -> d (a f)"))\
                    .then_inc(w1_in[parity], 16)
                if not first:
                    sp.wait_ge(yT_copied, i - 1)
                sp.dma_start(w2_t[:, parity, :].rearrange("p (a d) -> p a d", a=FT),
                             w2[bass.ds(e, 1), :, :].rearrange("o (a p) d -> p (o a) d", p=P))\
                    .then_inc(w2_in[parity], 16)
                sp.dma_start(b12_t[:, parity, :], b12[bass.ds(e, 1), :, :].rearrange("o p a -> p (o a)"))\
                    .then_inc(b_in[parity], 16)

            sp.wait_ge(zeros_made, 1)
            sp.dma_start(xs_dram.rearrange("(t p) d -> p t d", p=P),
                         row_st[:, 0, :].unsqueeze(1).to_broadcast([P, NTILES * SLOTS // P, D])).then_inc(zeros_stored, 16)

            def move_pair(j):
                for parity in range(2):
                    for c in range(NC):
                        move_max(j * 2 + parity, c, parity)

            with sp.Fori(0, SPLIT) as j:
                move_pair(j)
            move_max(2 * SPLIT, 0, 0)
            for k in range(TOPK):
                sp.wait_ge(rows_sent_k[k], 16 * NT)
            sp.wait_ge(routed, 1)
            over_tiles(sp, load_tile)
            move_max(2 * SPLIT, 1, 0)
            move_max(2 * SPLIT + 1, 0, 1)
            move_max(2 * SPLIT + 1, 1, 1)
            with sp.Fori(SPLIT + 1, PAIRS) as j:
                move_pair(j)
            def store(lo, hi):
                sp.dma_start(ov[:, lo:hi, :], acc[:, lo:hi, :]).then_inc(out_stored, 16)
            sp.wait_ge(rows_added, PAIRS - SPLIT - 1)
            sp.wait_ge(head_out_added, 4 * (NHEADS - H))
            store(0, NT - KT)
            sp.wait_ge(head_out_added, 4 * NHEADS - 2)
            store(NT - KT, NT - KT // 2)
            sp.wait_ge(head_out_added, 4 * NHEADS)
            store(NT - KT // 2, NT)
            sp.wait_ge(out_stored, 3 * 16)

        @block.gpsimd
        def _(pool):
            steps = [0]

            def link(ins):
                steps[0] += 1
                ins.then_inc(pool_done, 1)
                pool.wait_ge(pool_done, steps[0])
            pool.memset(prep[:, 0:2, :], 0.0).then_inc(prep_zeroed, 1)
            link(pool.memset(wq_cur[:, :, :].bitcast(FP32), 0.0))
            link(pool.memset(k_h1[KD:P, :].bitcast(FP32), 1.0))
            pool.memset(ckv[:, :, ONE:CW], 1.0).then_inc(ones_set, 1)
            pool.wait_ge(ones_set, 1)
            pool.memset(k_l1[KD:P, :].bitcast(FP32), 1.0).then_inc(ones_set, 1)
            pool.wait_ge(ones_set, 2)
            pool.memset(row_st[:, 0, :], 0.0).then_inc(zeros_made, 1)
            pool.wait_ge(zeros_made, 1)

            def query_weights(n, parity, first=False):
                pool.wait_ge(wq_made, 1)
                if not first:
                    pool.wait_ge(q_ready, n * 4 - 4)
                src = wq_abs[:, bass.ds(n % H, 1), :].rearrange("p a k -> p (a k)")
                pool.tensor_copy(wq_cur[:, parity, 0:KD], src[:, 0:KD]).then_inc(wq_current, 1)
                pool.tensor_copy(wq_cur[:, parity, KD:2 * KD], src[:, 0:KD]).then_inc(wq_current, 1)
                pool.tensor_copy(wq_cur[:, parity, P:P + KD + 1], src).then_inc(wq_current, 1)

            def keys(g, parity, first=False):
                if not first:
                    pool.wait_ge(k_low, NQ)
                    pool.wait_ge(context_added, g * 8 - 8)
                    pool.sem_inc(pool_waited, 1)
                b = g // H
                pool.tensor_copy(k_hh_cur[:, parity, :], k_hh[:, bass.ds(b * S, S)]).then_inc(keys_current, 1)
                pool.tensor_copy(k_l1_cur[:, parity, :], k_l1[:, bass.ds(b * S, S)]).then_inc(keys_current, 1)
                pool.tensor_copy(ckv_cur[:, parity, :],
                                 ckv[:, bass.ds(b * KT, KT), :].rearrange("p t c -> p (t c)"))\
                    .then_inc(keys_current, 1)

            pool.wait_ge(wq_made, 1)
            query_weights(0, 0, True)
            query_weights(1, 1, True)
            pool.wait_ge(k_low, 2)
            pool.wait_ge(c_copied, 2)
            keys(0, 0, True)
            keys(1, 1, True)
            query_weights(2, 0)
            pool.wait_ge(xn_ready, NQ)
            pool.wait_ge(consts_loaded, 16)
            pool.tensor_tensor(acc[:, :, :], acc[:, :, :], C["bo"].unsqueeze(1).to_broadcast([P, NT, D]), ALU.add)\
                .then_inc(bo_added, 1)

            def pair(j):
                new_batch = isinstance(j, int) and j % (H // 2) == 0
                query_weights(j * 2 + 1, 1)
                if new_batch:
                    keys(j * 2, 0)
                if not (isinstance(j, int) and j == PAIRS - 1):
                    query_weights(j * 2 + 2, 0)
                if new_batch:
                    keys(j * 2 + 1, 1)

            def dispatch(j, first=False):
                for t in range(DISPATCH):
                    for k in range(TOPK):
                        n = j * (DISPATCH * TOPK) + (t * TOPK + k)
                        if not (first and t == 0):
                            pool.wait_ge(routed, 1)
                            pool.wait_ge(rows_sent_k[k], (j * DISPATCH + t) * 16)
                        tt = bass.ds(j * DISPATCH + t, 1)
                        pool.tensor_copy(row_st[:, k, :], xn[:, tt, :].rearrange("p a d -> p (a d)"))\
                            .then_inc(staged, 1)
                        pool.tensor_copy(slot_st[:, k, :], slot_of[:, k, tt]).then_inc(staged, 1)
                        pool.wait_ge(staged, n * 2 + 2)
                        pool.sem_inc(pool_waited, 1)
                        pool.indirect_dma_start(
                            out=xs_dram, out_offset=bass.IndirectOffsetOnAxis(ap=slot_st[:, k, :], axis=0),
                            in_=row_st[:, k, :], in_offset=None).then_inc(rows_sent_k[k], 16)

            pair(1)
            pool.wait_ge(routed, 1)
            pool.wait_ge(zeros_stored, 16)
            dispatch(0, True)
            with pool.Fori(1, NT // DISPATCH - 1) as j:
                pair(j + 1)
                dispatch(j)
            pair(NT // DISPATCH)
            dispatch(NT // DISPATCH - 1)
            with pool.Fori(NT // DISPATCH + 1, SPLIT) as j:
                pair(j)
            pair(SPLIT)

            def store_tile(i, parity):
                pool.wait_ge(y_copied, i + 1)
                pool.dma_start(ys_dram[bass.ds(i * SLOTS, SLOTS), :].rearrange("(a p) d -> p a d", p=P),
                               y_out[:, parity, :, :]).then_inc(y_stored[parity], 16)

            over_tiles(pool, store_tile)
            pool.wait_ge(y_stored[0], (NTILES + 1) // 2 * 16)
            pool.wait_ge(y_stored[1], NTILES // 2 * 16)
            n_staged = NT * TOPK * 2

            def fetch(i):
                if not isinstance(i, int):
                    pool.wait_ge(routed, 1)
                    pool.wait_ge(rows_added, i)
                for t in range(COMBINE):
                    for k in range(TOPK):
                        at = t * TOPK + k
                        last = pool.tensor_copy(slot_st[:, at, :], slot_of[:, k, bass.ds(i * COMBINE + t, 1)])
                        last.then_inc(staged, 1)
                pool.wait_ge(y_stored[0], (NTILES + 1) // 2 * 16)
                pool.wait_ge(staged, i * (COMBINE * TOPK) + (n_staged + COMBINE * TOPK))
                pool.sem_inc(pool_waited, 1)
                for at in range(COMBINE * TOPK):
                    pool.indirect_dma_start(
                        out=fetched[:, at, :], out_offset=None, in_=ys_dram,
                        in_offset=bass.IndirectOffsetOnAxis(ap=slot_st[:, at, :], axis=0)).then_inc(rows_fetched, 16)

            fetch(0)
            new = list(range(SPLIT + 1, PAIRS - 1, H // 2))
            for at in new:
                pair(at)
                fetch(at - SPLIT)
                with pool.Fori(at + 1, min(at + H // 2, PAIRS - 1)) as j:
                    pair(j)
                    fetch(j - SPLIT)
            pair(PAIRS - 1)

        @block.scalar
        def _(act):
            def deviations(b):
                act.wait_ge(var_ready, b + 1)
                here = slice(b * KT, (b + 1) * KT)
                act.activation(rstd[:, 0, here], rstd[:, 1, here], ACT.Sqrt).then_inc(std_ready, 1)

            def xT_out(ck):
                act.wait_ge(xT_ready, ck + 1)
                if ck >= 2:
                    act.wait_ge(cg_ready, ck - 1)
                act.activation(xT_st[:, ck % 2, :], sc[0][:, ck % 2 * QC:(ck % 2 + 1) * QC], ACT.Copy)\
                    .then_inc(xT_copied, 1)

            def high_parts(ck):
                here = slice(ck * QC, (ck + 1) * QC)
                act.wait_ge(k_ready, ck + 1)
                act.activation(k_hh[:, here], sc[1][:, 0:QC], ACT.Identity, bias=b_k).then_inc(k_copied, 1)
                act.activation(k_h1[0:KD, here], sc[1][0:KD, 0:QC], ACT.Identity, bias=b_k[0:KD])\
                    .then_inc(k_top, 1)
                act.wait_ge(cq_ready, ck + 1)
                act.activation(xq[:, here], sc[1][:, QC:2 * QC], ACT.Identity, bias=b_cq).then_inc(cq_copied, 1)

            def beside(s):
                if s >= 2:
                    high_parts(s)
                if 1 <= s < NQ - 1:
                    xT_out(s + 1)
                if s in (1, 3):
                    deviations(s // 2 + 2)

            deviations(0)
            act.wait_ge(wT_ready, 1)
            act.wait_ge(prep_zeroed, 1)
            v2 = uv2.rearrange("p (h k) -> p h k", h=H)
            pv = cx[:, 0:H * 33].rearrange("p (h k) -> p h k", h=H)
            act.activation(ukT, mx[:, 512:512 + H * 33], ACT.Copy)
            act.activation(v2[:, :, 0:33], pv, ACT.Copy)
            act.activation(v2[:, :, 64:97], pv, ACT.Copy).then_inc(kv_made, 1)
            act.wait_ge(weights_loaded, 16)
            xT_out(0)
            xT_out(1)
            high_parts(0)
            high_parts(1)
            act.wait_ge(prod_ready, 2)
            act.activation(wvo[:, :, 0:D], mx.rearrange("p (h d) -> p h d", h=H), ACT.Copy).then_inc(wvo_made, 1)
            deviations(1)

            def gelus(i, parity):
                act.wait_ge(b_in[parity], (i // 2) * 16 + 16)
                if not (isinstance(i, int) and i < 2):
                    act.wait_ge(yT_ready, i - 1)
                for f in range(FT):
                    act.wait_ge(hidden_ready, i * FT + (f + 1))
                    act.activation(h_t[parity][:, f * SLOTS:(f + 1) * SLOTS], ps[:, f * 512:f * 512 + SLOTS],
                                   ACT.Gelu, bias=b12_t[:, parity, f:f + 1]).then_inc(hidden_done, 1)

            def experts():
                over_tiles(act, gelus)

            def q_high(n, c, parity):
                act.wait_ge(q_ready, n * 4 + (2 * c + 1))
                act.activation(q_hl[:, parity, c * QC:(c + 1) * QC], aux, ACT.Copy).then_inc(q_hi_done, 1)

            def q_one(n, c, parity):
                act.wait_ge(q_ready, n * 4 + (2 * c + 2))
                act.activation(q_h1[:, parity, c * QC:(c + 1) * QC], aux, ACT.Copy).then_inc(q_h1_done, 1)

            def context_out(g, c, first=False):
                act.wait_ge(context_added, g * 8 + (4 * c + 4))
                if not first:
                    act.wait_ge(head_out_ready, g * 4 + (2 * c - 2))
                act.activation(ctx_sb[:, c, :], cx, ACT.Copy).then_inc(context_copied, 1)

            def head(g, par, attend=True, ahead=2, first=False, second=False, late=None):
                for s in range(8):
                    if attend:
                        act.wait_ge(scores_ready, g * 8 + (s + 1))
                        if not (first and s < 4):
                            act.wait_ge(context_added, g * 8 + (s - 3))
                        act.activation(probs[:, s % 4, :], sc[s % 2], ACT.Exp, scale=SCALE)\
                            .then_inc(probs_ready, 1)
                    if first and s == 3:
                        act.wait_ge(gap_ready, 1)
                        act.activation(first_w[:, 1, :], first_w[:, 0, :], ACT.Exp).then_inc(gap_exp, 1)
                    if s == 0 and attend and not first:
                        context_out(g - 1, 1, second)
                    if s == 4 and attend:
                        context_out(g, 0, first)
                    if s == 1 and ahead >= 1:
                        q_high(g + 1, 1, 1 - par)
                    if s == 2 and ahead >= 1:
                        q_one(g + 1, 1, 1 - par)
                    if s == 5 and ahead >= 2:
                        q_high(g + 2, 0, par)
                    if s == 6 and ahead >= 2:
                        q_one(g + 2, 0, par)
                    if not attend:
                        beside(s)

            q_high(0, 0, 0)
            q_one(0, 0, 0)
            head(-1, 1, attend=False)
            run_heads(act, head, experts)
            context_out(NHEADS - 1, 1)

        @block.vector
        def _(dve):
            steps = [0]

            def link(ins):
                steps[0] += 1
                ins.then_inc(dve_done, 1)
                dve.wait_ge(dve_done, steps[0])

            std, var, r, r3 = (rstd[:, i, :] for i in range(4))

            def statistics(b):
                dve.wait_ge(x_loaded[b], 16)
                here = range(b * KT, (b + 1) * KT)
                for t in here:
                    last = dve.bn_stats(stat[:, t, :], acc[:, t, :])
                link(last)
                for t in here:
                    last = dve.bn_aggr(mv[:, t, :], stat[:, t, :])
                link(last)
                here = slice(b * KT, (b + 1) * KT)
                dve.tensor_scalar(var[:, here], mv[:, here, 1:2].rearrange("p t a -> p (t a)"), EPS, None, ALU.add)\
                    .then_inc(var_ready, 1)

            def inverses(b):
                v, y, e = (rstd[:, i, b * KT:(b + 1) * KT] for i in (1, 2, 3))
                dve.wait_ge(std_ready, b + 1)
                link(dve.reciprocal(y, rstd[:, 0, b * KT:(b + 1) * KT]))
                link(dve.tensor_tensor(e, y, y, ALU.mult))
                link(dve.tensor_tensor(e, e, v, ALU.mult))
                link(dve.tensor_scalar(e, e, -0.5, 1.5, ALU.mult, ALU.add))
                link(dve.tensor_tensor(y, y, e, ALU.mult))

            def normalise(ck):
                for t in range(ck * 4, ck * 4 + 4):
                    last = dve.tensor_scalar(xn[:, t, :], acc[:, t, :], mv[:, t, 0:1], r[:, t:t + 1],
                                             ALU.subtract, ALU.mult)
                last.then_inc(xn_ready, 1)

            def low_parts(ck):
                here = slice(ck * QC, (ck + 1) * QC)
                dve.wait_ge(k_top, ck + 1)
                dve.scalar_tensor_tensor(k_l1[0:KD, here], sc[1][0:KD, 0:QC], b_k[0:KD],
                                         k_hh[0:KD, here].bitcast(FP32), ALU.add, ALU.subtract)\
                    .then_inc(k_low, 1)
                dve.wait_ge(cq_copied, ck + 1)
                dve.scalar_tensor_tensor(xq[64:96, here], sc[1][64:96, QC:2 * QC], b_cq[64:96],
                                         xq[64:96, here].bitcast(FP32), ALU.add, ALU.subtract)\
                    .then_inc(cq_low, 1)
                dve.wait_ge(cg_ready, ck + 1)
                cg = cx[:, 0:4 * 64].rearrange("p (t k) -> p t k", t=4)
                tiles = slice(ck * 4, ck * 4 + 4)
                dve.tensor_copy(logits[:, tiles, :], cg[:, :, DC:DC + H])
                dve.tensor_tensor(ckv[:, tiles, 0:DC], cg[:, :, 0:DC],
                                  W["bkv"].unsqueeze(1).to_broadcast([P, 4, DC]), ALU.add).then_inc(c_copied, 1)

            def beside(s):
                if s >= 2:
                    low_parts(s)
                if s in (1, 3):
                    statistics(s // 2 + 2)
                if s in (2, 4):
                    inverses(s // 2 + 1)
                    normalise(s + 2)
                    normalise(s + 3)

            statistics(0)
            inverses(0)
            normalise(0)
            normalise(1)
            dve.wait_ge(wT_ready, 1)
            dve.wait_ge(prep_zeroed, 1)
            pq = mx[:, 0:H * 33].rearrange("p (h k) -> p h k", h=H)
            q3 = uq3.rearrange("p (h k) -> p h k", h=H)
            for g in range(3):
                dve.tensor_copy(q3[:, :, g * DC:(g + 1) * DC], pq[:, :, 0:DC])
            dve.tensor_copy(q3[:, :, 96:97], pq[:, :, DC:DC + 1])
            dve.tensor_copy(q3[:, :, 97:98], pq[:, :, DC:DC + 1]).then_inc(q3_made, 1)
            dve.wait_ge(weights_loaded, 16)
            f = fmat[:, 0:H * (KD + 1)].rearrange("p (h k) -> p h k", h=H)
            dve.tensor_copy(f[:, :, DC:KD], W["w_qr"].rearrange("p (h k) -> p h k", h=H))
            dve.tensor_copy(wvo[:, :, D:OW].rearrange("p h a -> p (h a)"), W["sum_rows"].to_broadcast([P, H]))
            dve.wait_ge(prod_ready, 1)
            pa = aux[:, 0:H * 33].rearrange("p (h k) -> p h k", h=H)
            dve.tensor_copy(f[:, :, 0:DC], pa[:, :, 0:DC])
            link(dve.tensor_copy(f[:, :, KD:KD + 1], pa[:, :, DC:DC + 1]))
            ff = fmat[:, 0:H * (KD + 1)]
            lo = uq3[:, 0:H * (KD + 1)]
            wqf = wq_abs[:, :, :].rearrange("p h k -> p (h k)")
            link(dve.tensor_copy(wqf, ff))
            link(dve.tensor_tensor(lo, ff, wqf.bitcast(FP32), ALU.subtract))
            link(dve.tensor_scalar(ff, wqf.bitcast(FP32), W["hi_rows"], None, ALU.mult))
            dve.scalar_tensor_tensor(wqf, lo, W["lo_rows"], ff, ALU.mult, ALU.add).then_inc(wq_made, 1)
            dve.wait_ge(ones_set, 1)
            low_parts(0)
            low_parts(1)
            statistics(1)

            TE = NT * E
            big = 1.7e38

            def rt(i, n=TE):
                return prep[:, i // 4, (i % 4) * TE:(i % 4) * TE + n]

            def te(v):
                return v.rearrange("p (t e) -> p t e", e=E)

            def over_e(v):
                return v.unsqueeze(2).to_broadcast([P, NT, E])
            one_hot = [rt(0), rt(1)]
            work, rest, both, pre, tot_a, tot_b = (rt(i) for i in range(2, 8))
            small = rt(8)
            best = [small[:, 0:NT], small[:, NT:2 * NT]]
            pick = small[:, 2 * NT:3 * NT]
            fall = C["falling"].unsqueeze(1).to_broadcast([P, NT, E])
            tiles_i = rt(9, E).bitcast(I32)
            cum = [rt(10, E), rt(11, E)]
            tiles = rt(12 - 1, 2 * E)[:, E:2 * E]

            def mark_best(k, src):
                link(dve.reduce_max(best[k], src, AX.X))
                link(dve.tensor_tensor(te(work), src, over_e(best[k]), ALU.is_equal))

            def choose(k):
                link(dve.tensor_tensor(te(work), te(work), fall, ALU.mult))
                link(dve.reduce_max(pick, te(work), AX.X))
                link(dve.tensor_tensor(te(one_hot[k]), fall, over_e(pick), ALU.is_equal))

            def running_sum(src, dst, step, n):
                link(dve.tensor_copy(dst[:, 0:step], src[:, 0:step]))
                link(dve.tensor_tensor(dst[:, step:n], src[:, step:n], src[:, 0:n - step], ALU.add))

            def slots(k):
                link(dve.tensor_tensor(work, one_hot[k], pre, ALU.mult))
                link(dve.reduce_sum(pick, te(work), AX.X))
                return dve.tensor_copy(slot_of[:, k, :], pick)

            def route(step):
                if step == 0:
                    dve.wait_ge(wvo_made, 1)
                    dve.wait_ge(consts_loaded, 16)
                    dve.wait_ge(c_copied, NQ)
                    mark_best(0, logits[:, :, :])
                    choose(0)
                if step == 1:
                    link(dve.tensor_scalar(work, one_hot[0], -2 * big, big, ALU.mult, ALU.add))
                    link(dve.tensor_tensor(te(rest), logits[:, :, :], te(work), ALU.min))
                    mark_best(1, te(rest))
                if step == 2:
                    choose(1)
                    dve.tensor_tensor(both, one_hot[0], one_hot[1], ALU.add).then_inc(chosen, 1)
                    dve.tensor_tensor(first_w[:, 0, :], best[1], best[0], ALU.subtract).then_inc(gap_ready, 1)
                if step == 4:
                    dve.wait_ge(gap_exp, 1)
                    link(dve.tensor_scalar(best[0], first_w[:, 1, :], 1.0, None, ALU.add))
                    link(dve.reciprocal(first_w[:, 0, :], best[0]))
                    link(dve.tensor_tensor(first_w[:, 1, :], first_w[:, 1, :], first_w[:, 0, :], ALU.mult))
                    dve.wait_ge(counted, 1)
                    link(dve.tensor_copy(pre, aux[:, 0:TE]))
                    dve.tensor_copy(tot_a, aux[:, TE:2 * TE]).then_inc(counts_taken, 1)
                    dve.wait_ge(counts_taken, 1)
                if step == 5:
                    link(dve.tensor_tensor(pre, pre, tot_a, ALU.subtract))
                    running_sum(tot_a, tot_b, E, TE)
                if step == 6:
                    running_sum(tot_b, tot_a, 2 * E, TE)
                    running_sum(tot_a, tot_b, 4 * E, TE)
                if step == 7:
                    running_sum(tot_b, tot_a, 8 * E, TE)
                    running_sum(tot_a, tot_b, 16 * E, TE)
                if step == 8:
                    link(dve.tensor_tensor(pre, pre, tot_b, ALU.add))
                    link(dve.tensor_scalar(cum[0], tot_b[:, TE - E:TE], float(SLOTS - 1), None, ALU.add))
                    link(dve.tensor_copy(tiles_i, cum[0]))
                    link(dve.tensor_scalar(tiles_i, tiles_i, SLOTS.bit_length() - 1, None, ALU.arith_shift_right))
                if step == 9:
                    link(dve.tensor_copy(cum[0], tiles_i))
                    link(dve.tensor_copy(tiles, cum[0]))
                    running_sum(cum[0], cum[1], 1, E)
                    running_sum(cum[1], cum[0], 2, E)
                    running_sum(cum[0], cum[1], 4, E)
                if step == 10:
                    cmp_ = fetched[:, 0:3, :].rearrange("p a d -> p (a d)")[:, 0:NTILES * E]\
                        .rearrange("p (t e) -> p t e", e=E)
                    link(dve.tensor_tensor(cmp_, C["tile_no"].unsqueeze(2).to_broadcast([P, NTILES, E]),
                                           cum[1].unsqueeze(1).to_broadcast([P, NTILES, E]), ALU.is_ge))
                    link(dve.reduce_sum(work[:, 0:NTILES], cmp_, AX.X))
                    link(dve.tensor_scalar(expert_of[:, :], work[:, 0:NTILES], float(E - 1), None, ALU.min))
                if step == 11:
                    first_slot = rest[:, 0:E]
                    link(dve.tensor_tensor(first_slot, cum[1], tiles, ALU.subtract))
                    link(dve.tensor_scalar(first_slot, first_slot, float(SLOTS), None, ALU.mult))
                    link(dve.tensor_tensor(te(pre), te(pre), first_slot.unsqueeze(1).to_broadcast([P, NT, E]), ALU.add))
                if step == 12:
                    link(slots(0))
                if step == 13:
                    slots(1).then_inc(routed, 1)

            def slots_transposed(i, parity):
                dve.wait_ge(xgT_ready, i + 1)
                dve.tensor_copy(xgT[:, parity, :], mx[:, 0:SLOTS]).then_inc(xgT_copied, 1)

            def outputs(i, parity):
                dve.wait_ge(yT_ready, i + 1)
                if not (isinstance(i, int) and i == 0):
                    dve.wait_ge(y_ready, i)
                dve.tensor_scalar(yT, mx[:, 512:512 + SLOTS], b12_t[:, parity, FT:FT + 1], None, ALU.add)\
                    .then_inc(yT_copied, 1)
                dve.wait_ge(y_ready, i + 1)
                if not (isinstance(i, int) and i < 2):
                    dve.wait_ge(y_stored[parity], (i // 2) * 16)
                dve.tensor_copy(y_out[:, parity, :, :].rearrange("p a d -> p (a d)"), aux[:, 0:SLOTS])\
                    .then_inc(y_copied, 1)

            def experts():
                def tile(i, parity):
                    if not (isinstance(i, int) and i == NTILES - 1):
                        slots_transposed(i + 1, 1 - parity)
                    outputs(i, parity)
                slots_transposed(0, 0)
                over_tiles(dve, tile)

            def add_experts(i):
                dve.wait_ge(rows_fetched, i * (16 * COMBINE * TOPK) + 16 * COMBINE * TOPK)
                for k in range(TOPK):
                    if k:
                        dve.wait_ge(half_added, i + 1)
                    for t in range(COMBINE):
                        tt = bass.ds(i * COMBINE + t, 1)
                        a = acc[:, tt, :].rearrange("p a d -> p (a d)")
                        last = dve.scalar_tensor_tensor(a, fetched[:, t * TOPK + k, :], first_w[:, k, tt], a,
                                                        ALU.mult, ALU.add)
                    last.then_inc(rows_added if k else half_added, 1)

            def q_low(n, c, parity):
                dve.wait_ge(q_hi_done, n * 2 + (c + 1))
                lo_part = q_hl[KD:P, parity, c * QC:(c + 1) * QC]
                dve.tensor_tensor(lo_part, aux[KD:P, :], lo_part.bitcast(FP32), ALU.subtract)\
                    .then_inc(q_lo_done, 1)

            def add_out(g, c, half):
                dve.wait_ge(head_out_ready, g * 4 + (2 * c + half + 1))
                o = aux[:, 0:2 * OW].rearrange("p (t k) -> p t k", t=2)
                dve.reciprocal(rsum[:, half, :], o[:, :, D:OW].rearrange("p t a -> p (t a)")).then_inc(recip_done, 1)
                dve.wait_ge(recip_done, g * 4 + (2 * c + half + 1))
                b = g // H
                for t in range(2):
                    a = acc[:, bass.ds(b * KT + (c * 4 + half * 2 + t), 1), :].rearrange("p a d -> p (a d)")
                    last = dve.scalar_tensor_tensor(a, o[:, t, 0:D], rsum[:, half, t:t + 1], a, ALU.mult, ALU.add)
                last.then_inc(head_out_added, 1)

            def max_rows(n, c, first=False):
                dve.wait_ge(maxT_ready, n * 2 + (c + 1))
                if not first:
                    dve.wait_ge(mrow_moved[c], n * 16)
                dve.tensor_scalar(mrow[:, c, :], mx[0:4, 0:P], -1.0, None, ALU.mult).then_inc(mrow_ready, 1)

            def head(g, par, attend=True, ahead=2, first=False, second=False, late=None):
                for s in range(8):
                    if s == 0 and attend:
                        max_rows(g, 1, first)
                    if s == 4 and ahead >= 1:
                        max_rows(g + 1, 0, not attend)
                    if attend and not first:
                        if s == 0:
                            add_out(g - 1, 0, 1)
                        if s in (3, 4):
                            add_out(g - 1, 1, s - 3)
                    if s == 1 and ahead >= 1:
                        q_low(g + 1, 1, 1 - par)
                    if s == 5 and ahead >= 2:
                        q_low(g + 2, 0, par)
                    if s == 7 and attend:
                        if first:
                            dve.wait_ge(bo_added, 1)
                        add_out(g, 0, 0)
                    if s == 6 and par == 1 and late is not None:
                        add_experts(late)
                    if ahead >= 1:
                        dve.wait_ge(max_ready, g * 8 + (9 + s))
                        dve.reduce_max(mcol[:, 1 - par, s:s + 1], mx, AX.X).then_inc(max_done, 1)
                    if not attend:
                        beside(s)
                    if first or second:
                        route(s + 8 * second)

            q_low(0, 0, 0)
            inverses(1)
            normalise(2)
            normalise(3)
            head(-1, 1, attend=False)
            run_heads(dve, head, experts)
            add_out(NHEADS - 1, 0, 1)
            add_out(NHEADS - 1, 1, 0)
            add_out(NHEADS - 1, 1, 1)

        @block.tensor
        def _(pe):
            pe.wait_ge(weights_loaded, 16)
            pe.wait_ge(up_loaded, 16)
            for i, dst in enumerate((mx[:, 0:264], mx[:, 512:776], cx[:, 0:264])):
                for h in range(H):
                    last = pe.transpose(dst[:, h * 33:(h + 1) * 33], up33[:, i, h * DK:(h + 1) * DK], ident[0:33, 0:33])
            last.then_inc(wT_ready, 1)

            def x_transposed(ck):
                pe.wait_ge(xn_ready, ck + 1)
                if ck >= 2:
                    pe.wait_ge(xT_copied, ck - 1)
                for t in range(4):
                    o = ck % 2 * QC + t * P
                    last = pe.transpose(sc[0][:, o:o + P], xn[:, ck * 4 + t, :], ident)
                last.then_inc(xT_ready, 1)

            def latents(ck):
                xT = xT_st[:, ck % 2, :]
                pe.wait_ge(xT_copied, ck + 1)
                if ck > 0:
                    pe.wait_ge(k_low, ck)
                pe.matmul(sc[1][:, 0:QC], w_k2, xT, start=True, stop=True).then_inc(k_ready, 1)
                if ck > 0:
                    pe.wait_ge(cq_low, ck)
                pe.matmul(sc[1][:, QC:2 * QC], w_cq, xT, start=True, stop=True).then_inc(cq_ready, 1)
                if ck > 0:
                    pe.wait_ge(c_copied, ck)
                for t in range(4):
                    last = pe.matmul(cx[:, t * 64:t * 64 + DC + H], xT[:, t * P:(t + 1) * P],
                                     w_cg, start=True, stop=True)
                last.then_inc(cg_ready, 1)

            def beside(s):
                if s >= 2:
                    latents(s)
                if 1 <= s < NQ - 1:
                    x_transposed(s + 1)

            x_transposed(0)
            x_transposed(1)
            pe.wait_ge(q3_made, 1)
            pe.wait_ge(kv_made, 1)
            for h in range(H):
                last = pe.matmul(aux[:, h * 33:(h + 1) * 33], uq3[:, h * P:(h + 1) * P],
                                 ukT[:, h * 33:(h + 1) * 33], start=True, stop=True)
            last.then_inc(prod_ready, 1)
            latents(0)
            latents(1)
            pe.wait_ge(wo_loaded, 16)
            for h in range(H):
                last = pe.matmul(mx[:, h * D:(h + 1) * D], uv2[:, h * P:(h + 1) * P],
                                 wo_sb[:, h, :], start=True, stop=True)
            last.then_inc(prod_ready, 1)

            def query(n, c, form, parity):
                pe.wait_ge(wq_current, n * 3 + 3)
                pe.matmul(aux, wq_cur[:, parity, form * P:(form + 1) * P],
                          xq[:, bass.ds((n // H) * S + c * QC, QC)], start=True, stop=True).then_inc(q_ready, 1)

            def head_out(g, c, half):
                h = g % H
                pe.wait_ge(context_copied, g * 2 + (c + 1))
                for t in range(2):
                    i = half * 2 + t
                    last = pe.matmul(aux[:, t * OW:(t + 1) * OW], ctx_sb[:, c, i * P:(i + 1) * P],
                                     wvo[:, bass.ds(h, 1), :].rearrange("p a k -> p (a k)"), start=True, stop=True)
                last.then_inc(head_out_ready, 1)

            def fill(g, s, par, attend, ahead, first):
                before = attend and not first
                if s == 0 and before:
                    pe.wait_ge(head_out_added, g * 4 - 3)
                    head_out(g - 1, 0, 1)
                if s == 1 and ahead >= 1:
                    if before:
                        pe.wait_ge(head_out_added, g * 4 - 2)
                    else:
                        pe.wait_ge(q_h1_done, g * 2 + 3)
                    query(g + 1, 1, 0, 1 - par)
                if s == 2 and ahead >= 1:
                    pe.wait_ge(q_lo_done, g * 2 + 4)
                    query(g + 1, 1, 1, 1 - par)
                if s == 4 and first:
                    pe.wait_ge(q_h1_done, g * 2 + 4)
                    pe.wait_ge(consts_loaded, 16)
                    pe.wait_ge(chosen, 1)
                    both = prep[:, 1, 0:NT * E]
                    pe.matmul(aux[:, 0:NT * E], C["upper"], both, start=True, stop=True)
                    pe.matmul(aux[:, NT * E:2 * NT * E], C["ones"], both, start=True, stop=True).then_inc(counted, 1)
                if s == 3 and before:
                    if ahead >= 1:
                        pe.wait_ge(q_h1_done, g * 2 + 4)
                    else:
                        pe.wait_ge(head_out_added, g * 4 - 2)
                    head_out(g - 1, 1, 0)
                if s == 4 and before:
                    pe.wait_ge(head_out_added, g * 4 - 1)
                    head_out(g - 1, 1, 1)
                if s == 5 and ahead >= 2:
                    if before:
                        pe.wait_ge(head_out_added, g * 4)
                    elif first:
                        pe.wait_ge(counts_taken, 1)
                    else:
                        pe.wait_ge(q_h1_done, g * 2 + 4)
                    query(g + 2, 0, 0, par)
                if s == 6 and ahead >= 2:
                    pe.wait_ge(q_lo_done, g * 2 + 5)
                    query(g + 2, 0, 1, par)
                if s == 7 and attend:
                    if ahead >= 2:
                        pe.wait_ge(q_h1_done, g * 2 + 5)
                    else:
                        pe.wait_ge(head_out_added, g * 4)
                    head_out(g, 0, 0)

            def add_context(g, s, par, first_unit=False):
                c, p = s // 4, s % 4
                pe.wait_ge(probs_ready, g * 8 + (s + 1))
                if p == 0 and not first_unit:
                    pe.wait_ge(context_copied, g * 2 + c)
                for i in range(2):
                    kt = 2 * p + i
                    last = pe.matmul(cx[CW * i:CW * (i + 1), :], ckv_cur[:, par, kt * CW:(kt + 1) * CW],
                                     probs[:, s % 4, i * QC:(i + 1) * QC], start=(p == 0), stop=(p == 3))
                last.then_inc(context_added, 1)

            def head(g, par, attend=True, ahead=2, first=False, second=False, late=None):
                for s in range(8):
                    c, p = s // 4, s % 4
                    if attend:
                        if s == 0:
                            pe.wait_ge(keys_current, (g // H) * 6 + (3 * par + 3))
                        if p == 0:
                            pe.wait_ge(q_lo_done, g * 2 + (c + 1))
                            pe.wait_ge(mrow_moved[c], g * 16 + 16)
                        if not (first and s < 2):
                            pe.wait_ge(probs_ready, g * 8 + (s - 1))
                        for i in range(2):
                            kt = 2 * p + i
                            o = sc[s % 2][:, i * QC:(i + 1) * QC]
                            pe.matmul(o, k_hh_cur[:, par, kt * P:(kt + 1) * P], q_hl[:, par, c * QC:(c + 1) * QC],
                                      start=True, stop=False)
                            last = pe.matmul(o, k_l1_cur[:, par, kt * P:(kt + 1) * P],
                                             q_h1[:, par, c * QC:(c + 1) * QC], start=False, stop=True)
                        last.then_inc(scores_ready, 1)
                    fill(g, s, par, attend, ahead, first)
                    if s == 0 and attend:
                        transpose_max(g, 1, par)
                    if s == 4 and ahead >= 1:
                        transpose_max(g + 1, 0, 1 - par)
                    if attend:
                        if s > 0:
                            add_context(g, s - 1, par, first and s == 1)
                        elif not first:
                            add_context(g - 1, 7, 1 - par)
                    if ahead >= 1:
                        if s in (0, 4):
                            pe.wait_ge(q_h1_done, g * 2 + (3 + s // 4))
                            if attend or s == 4:
                                pe.wait_ge(mrow_ready, g * 2 + (2 + s // 4))
                        else:
                            pe.wait_ge(max_done, g * 8 + (8 + s))
                        for i in range(2):
                            last = pe.matmul(mx[:, i * QC:(i + 1) * QC], q_h1[:, 1 - par, s * P:(s + 1) * P],
                                             k_h1[:, bass.ds(((g + 1) // H) * S + i * QC, QC)],
                                             start=True, stop=True)
                        last.then_inc(max_ready, 1)
                    if not attend:
                        beside(s)

            def transpose_max(n, c, parity):
                pe.wait_ge(max_done, n * 8 + (4 * c + 4))
                pe.transpose(mx[0:4, 0:P], mcol[:, parity, 4 * c:4 * c + 4], ident).then_inc(maxT_ready, 1)

            def slots_in(i, parity):
                pe.wait_ge(x_in[parity], (i // 2) * 16 + 16)
                if not (isinstance(i, int) and i == 0):
                    pe.wait_ge(xgT_copied, i)
                for a in range(2):
                    last = pe.transpose(mx[:, a * P:(a + 1) * P], xg[:, parity, a, :], ident)
                last.then_inc(xgT_ready, 1)

            def hidden(i, parity):
                pe.wait_ge(w1_in[parity], (i // 2) * 16 + 16)
                pe.wait_ge(xgT_copied, i + 1)
                for f in range(FT):
                    pe.matmul(ps[:, f * 512:f * 512 + SLOTS], w1_t[:, parity, f * P:(f + 1) * P],
                              xgT[:, parity, :], start=True, stop=True).then_inc(hidden_ready, 1)

            def output(i, parity):
                pe.wait_ge(w2_in[parity], (i // 2) * 16 + 16)
                if not (isinstance(i, int) and i == 0):
                    pe.wait_ge(yT_copied, i)
                for f in range(FT):
                    pe.wait_ge(hidden_done, i * FT + (f + 1))
                    last = pe.matmul(mx[:, 512:512 + SLOTS], w2_t[:, parity, f * P:(f + 1) * P],
                                     h_t[parity][:, f * SLOTS:(f + 1) * SLOTS], start=(f == 0), stop=(f == FT - 1))
                last.then_inc(yT_ready, 1)

            def slots_out(i, parity):
                pe.wait_ge(yT_copied, i + 1)
                if not (isinstance(i, int) and i == 0):
                    pe.wait_ge(y_copied, i)
                for a in range(2):
                    last = pe.transpose(aux[:, a * P:(a + 1) * P], yT[:, a * P:(a + 1) * P], ident)
                last.then_inc(y_ready, 1)

            def experts():
                pe.wait_ge(probs_ready, SPLIT * 16)
                pe.wait_ge(max_done, SPLIT * 16 + 8)
                pe.wait_ge(head_out_added, SPLIT * 8 - 3)

                def tile(i, parity):
                    last = isinstance(i, int) and i == NTILES - 1
                    if not last:
                        slots_in(i + 1, 1 - parity)
                    output(i, parity)
                    if not last:
                        hidden(i + 1, 1 - parity)
                    slots_out(i, parity)
                slots_in(0, 0)
                hidden(0, 0)
                over_tiles(pe, tile)
                pe.wait_ge(y_copied, NTILES)

            pe.wait_ge(cq_low, 1)
            query(0, 0, 0, 0)
            pe.wait_ge(q_lo_done, 1)
            query(0, 0, 1, 0)
            pe.wait_ge(wvo_made, 1)
            head(-1, 1, attend=False)
            pe.wait_ge(k_low, NQ)
            pe.wait_ge(cq_low, NQ)
            pe.wait_ge(c_copied, NQ)
            run_heads(pe, head, experts)
            last_head = NHEADS - 1
            add_context(last_head, 7, 1)
            pe.wait_ge(head_out_added, 4 * last_head + 1)
            head_out(last_head, 0, 1)
            pe.wait_ge(head_out_added, 4 * last_head + 2)
            head_out(last_head, 1, 0)
            pe.wait_ge(head_out_added, 4 * last_head + 3)
            head_out(last_head, 1, 1)


def layout(inputs):
    import numpy as np
    a = {name.split("_", 2)[2]: np.asarray(v) for name, v in inputs.items()}
    f32 = np.float32

    def zeros(rows, cols):
        return np.zeros((rows, cols), f32)

    def rows_marked(*ranges):
        mask = zeros(P, 1)
        for lo, hi in ranges:
            mask[lo:hi] = 1
        return mask
    up = np.stack([np.concatenate([a["W_" + n], a["b_" + n][None]]) for n in ("UQ", "UK", "UV")], axis=1)
    key = [a["W_DKV"], a["W_KR"]]
    key_bias = [a["b_DKV"], a["b_KR"]]
    w = {
        "ident": np.eye(P, dtype=f32),
        "w_k2": np.concatenate(key + key, axis=1),
        "w_cq": np.concatenate([a["W_DQ"]] * 3 + [zeros(D, P - 3 * DC)], axis=1),
        "w_cg": np.concatenate([a["W_DKV"], a["gate_w"]], axis=1),
        "w_qr": np.concatenate([a["W_QR"]] * 3 + [a["b_QR"][None]] * 2 + [zeros(P - 3 * DC - 2, H * DR)]),
        "bkv": np.repeat(a["b_DKV"][None], P, axis=0),
        "b_k": np.concatenate(key_bias + key_bias)[:, None],
        "b_cq": np.concatenate([a["b_DQ"]] * 3 + [np.ones(P - 3 * DC, f32)])[:, None],
        "hi_rows": rows_marked((0, DC), (2 * DC, 3 * DC + 1)),
        "lo_rows": rows_marked((DC, 2 * DC), (3 * DC + 1, 3 * DC + 2)),
        "sum_rows": rows_marked((ONE, ONE + 1), (CW + ONE, CW + ONE + 1)),
    }
    c = {
        "bo": np.repeat(a["b_O"][None], P, axis=0),
        "upper": np.triu(np.ones((P, P), f32), 1),
        "ones": np.ones((P, P), f32),
        "falling": np.repeat(np.arange(E, 0, -1, dtype=f32)[None], P, axis=0),
        "tile_no": np.repeat(np.arange(NTILES, dtype=f32)[None], P, axis=0),
    }
    assert list(w) == list(W_COLS) and list(c) == list(C_COLS)
    b1 = a["b1"].reshape(E, FT, P).transpose(0, 2, 1)
    arrays = {
        "x": a["h_t"], "up": up, "weights": np.concatenate(list(w.values()), axis=1), "wo": a["W_O"],
        "consts": np.concatenate(list(c.values()), axis=1), "w1": a["w1"], "w2": a["w2"],
        "b12": np.concatenate([b1, a["b2"].reshape(E, P, 1)], axis=2),
    }
    return {name: np.ascontiguousarray(v) for name, v in arrays.items()}


def kernel(**inputs):
    import concourse.bacc as bacc
    from concourse.bass_utils import run_bass_kernel_spmd

    nc = bacc.Bacc("TRN2", target_bir_lowering=False, num_devices=1)
    arrays = layout(inputs)
    args = [nc.dram_tensor(name, a.shape, mybir.dt.from_np(a.dtype), kind="ExternalInput").ap()
            for name, a in arrays.items()]
    args.append(nc.dram_tensor("out", (B, S, D), FP32, kind="ExternalOutput").ap())
    moe_transformer_layer(nc, *args)
    r = run_bass_kernel_spmd(nc, [arrays], core_ids=[0])
    return r.results[0]["out"]
```

```python
import concourse.bass as bass
from concourse import mybir
from contextlib import ExitStack

FP32 = mybir.dt.float32
FP32R = mybir.dt.float32r
U32 = mybir.dt.uint32
I32 = mybir.dt.int32
ALU = mybir.AluOpType
ACT = mybir.ActivationFunctionType
AX = mybir.AxisListType

P = 128
B, S, D = 4, 1024, 128
H, DK, DC, DR = 8, 128, 32, 32
NT = B * S // P
QC = 512
NC = S // QC
KT = S // P
NQ = B * S // QC
SCALE = 1.0 / (DK + DR) ** 0.5
EPS = 1e-5
KD = DC + DR
ROW_MAX = KD + 1
UP = DC + 1
CW = 64
ONE = DC
OW = D + 1
NHEADS = B * H
F, E, TOPK = 512, 8, 2
FT = F // P
NTOK = B * S
SLOTS = 256
NTILES = (NTOK * TOPK + E * (SLOTS - 1)) // SLOTS
PAIRS = NHEADS // 2
SPLIT = 7
DISPATCH = 8
COMBINE = NT // (PAIRS - SPLIT - 1)

W_COLS = {"ident": P, "w_k2": P, "w_cq": P, "w_cg": DC + H, "w_q": H * (KD + 1), "bkv": DC,
          "b_k": 1, "b_cq": 1, "hi_rows": 1, "lo_rows": 1, "sum_rows": 1}
C_COLS = {"bo": D, "upper": P, "ones": P, "falling": E, "tile_no": NTILES}


def columns(packed, widths):
    parts, at = {}, 0
    for name, width in widths.items():
        parts[name] = packed[:, at:at + width]
        at += width
    return parts


def moe_transformer_layer(nc, x, up, weights, wo, consts, w1, w2, b12, out):
    with ExitStack() as ctx:
        def sb(name, shape, dt=FP32):
            return ctx.enter_context(nc.sbuf_tensor(name, shape, dt))

        def sem(name):
            return ctx.enter_context(nc.semaphore(name))

        acc = sb("acc", [P, NT, D])
        xT_st = sb("xT_st", [P, 2, QC])
        xq = sb("xq", [P, B * S], FP32R)
        k_hh = sb("k_hh", [P, B * S], FP32R)
        k_h1 = sb("k_h1", [P, B * S], FP32R)
        k_l1 = sb("k_l1", [P, B * S], FP32R)
        ckv = sb("ckv", [P, NT, CW])
        logits = sb("logits", [P, NT, H])
        wq_abs = sb("wq_abs", [P, H, KD + 1], FP32R)
        wvo = sb("wvo", [P, H, OW])
        packed_w = sb("packed_w", [P, sum(W_COLS.values())])
        packed_c = sb("packed_c", [P, sum(C_COLS.values())])
        W, C = columns(packed_w, W_COLS), columns(packed_c, C_COLS)
        ident, w_k2, w_cq, w_cg, b_k, b_cq = (W[n] for n in ("ident", "w_k2", "w_cq", "w_cg", "b_k", "b_cq"))
        wq_cur = sb("wq_cur", [P, 2, P], FP32R)
        k_hh_cur = sb("k_hh_cur", [P, 2, S], FP32R)
        k_l1_cur = sb("k_l1_cur", [P, 2, S], FP32R)
        ckv_cur = sb("ckv_cur", [P, 2, KT * CW])
        q_hl = sb("q_hl", [P, 2, S], FP32R)
        q_h1 = sb("q_h1", [P, 2, S], FP32R)
        mcol = sb("mcol", [P, 2, KT])
        mrow = sb("mrow", [4, 2, P], FP32R)
        ctx_sb = sb("ctx_sb", [P, 2, QC])
        rsum = sb("rsum", [P, 2, 2])
        spare = sb("spare", [P, 2])
        probs = sb("probs", [P, 4, 2 * QC])
        stat = sb("stat", [P, NT, 6])
        mv = sb("mv", [P, NT, 2])
        rstd = sb("rstd", [P, 4, NT])

        first_w = sb("first_w", [P, 2, NT])
        slot_of = sb("slot_of", [P, 2, NT], U32)
        expert_of = sb("expert_of", [P, NTILES], U32)
        slot_st = sb("slot_st", [P, 2 * COMBINE, 1], U32)
        row_st = sb("row_st", [P, 2, D])
        fetched = sb("fetched", [P, 2 * COMBINE, D])

        xs_dram = nc.dram_tensor("x_sorted", (NTILES * SLOTS, D), FP32).ap()
        ys_dram = nc.dram_tensor("y_sorted", (NTILES * SLOTS, D), FP32).ap()

        ps = ctx.enter_context(nc.psum_tensor("ps", [P, 8 * 512], FP32))
        sc = [ps[:, 1024 * i:1024 * (i + 1)] for i in range(2)]
        mx = ps[:, 2048:3072]
        cx = ps[:, 3072:3584]
        aux = ps[:, 3584:4096]

        up_w = probs[0:DC + 1, :, :].rearrange("p a b -> p (a b)")[:, 0:3 * H * DK + DC + 1]
        wo_sb = sb("wo_sb", [P, H, D])
        prep = sb("prep", [P, 3, H * P])
        uq3, uv2 = prep[:, 0, :], prep[:, 1, :]
        w1_t = prep[:, 0:1, :].rearrange("p a (b f) -> p (a b) f", b=2)
        w2_t = prep[:, 1:2, :].rearrange("p a (b f) -> p (a b) f", b=2)
        h_t = [prep[:, 2, :], wo_sb[:, :, :].rearrange("p h d -> p (h d)")]
        xg = sb("xg", [P, 2, 2, D])
        y_out = sb("y_out", [P, 2, 2, D])
        yT = xT_st[:, 0, SLOTS:2 * SLOTS]
        b12_t = sb("b12_t", [P, 2, FT + 1])
        ukT = ctx_sb[:, 0, 0:H * UP]
        with nc.sbuf_tensor("xn", [P, NT, D], FP32) as xn:
            pass
        w1_hl = sb("w1_hl", [P, 2, 2, F], FP32R)
        xgT = sb("xgT", [P, 2, 2, SLOTS], FP32R)

        x_loaded = [sem(f"x_loaded{i}") for i in range(B)]
        up_loaded = sem("up_loaded")
        weights_loaded = sem("weights_loaded")
        wo_loaded = sem("wo_loaded")
        consts_loaded = sem("consts_loaded")
        prep_zeroed = sem("prep_zeroed")
        ones_set = sem("ones_set")
        zeros_made = sem("zeros_made")
        pool_done = sem("pool_done")
        dve_done = sem("dve_done")
        var_ready = sem("var_ready")
        std_ready = sem("std_ready")
        rstd_ready = sem("rstd_ready")
        xn_ready = sem("xn_ready")
        wT_ready = sem("wT_ready")
        qk_made = sem("qk_made")
        v2_made = sem("v2_made")
        prod_ready = sem("prod_ready")
        wq_made = sem("wq_made")
        wvo_made = sem("wvo_made")
        xT_ready = sem("xT_ready")
        xT_copied = sem("xT_copied")
        k_ready = sem("k_ready")
        cq_ready = sem("cq_ready")
        cg_ready = sem("cg_ready")
        k_low = sem("k_low")
        cq_copied = sem("cq_copied")
        cq_low = sem("cq_low")
        c_copied = sem("c_copied")
        k_top = sem("k_top")
        bo_added = sem("bo_added")
        counts_taken = sem("counts_taken")
        zeros_stored = sem("zeros_stored")
        gap_ready = sem("gap_ready")
        gap_exp = sem("gap_exp")
        chosen = sem("chosen")
        counted = sem("counted")
        routed = sem("routed")
        staged = sem("staged")
        pool_waited = sem("pool_waited")
        rows_sent_k = [sem(f"rows_sent{k}") for k in range(TOPK)]
        rows_fetched = sem("rows_fetched")
        rows_added = sem("rows_added")
        half_added = sem("half_added")
        x_in = [sem(f"slots_loaded{i}") for i in range(2)]
        w1_in = [sem(f"w1_loaded{i}") for i in range(2)]
        w2_in = [sem(f"w2_loaded{i}") for i in range(2)]
        b_in = [sem(f"expert_biases_loaded{i}") for i in range(2)]
        xgT_ready = sem("xgT_ready")
        xgT_copied = sem("xgT_copied")
        xgT_high = sem("xgT_high")
        w1_high = sem("w1_high")
        w1_split = sem("w1_split")
        hidden_ready = sem("hidden_ready")
        hidden_done = sem("hidden_done")
        yT_ready = sem("yT_ready")
        yT_copied = sem("yT_copied")
        y_ready = sem("y_ready")
        y_copied = sem("y_copied")
        y_stored = [sem(f"y_stored{i}") for i in range(2)]
        scores_ready = sem("scores_ready")
        probs_ready = sem("probs_ready")
        context_added = sem("context_added")
        context_copied = sem("context_copied")
        max_ready = sem("max_ready")
        max_done = sem("max_done")
        maxT_ready = sem("maxT_ready")
        mrow_ready = sem("mrow_ready")
        mrow_moved = [sem(f"mrow_moved{c}") for c in range(2)]
        q_ready = sem("q_ready")
        q_hi_done = sem("q_hi_done")
        q_lo_done = sem("q_lo_done")
        q_h1_done = sem("q_h1_done")
        head_out_ready = sem("head_out_ready")
        recip_done = sem("recip_done")
        head_out_added = sem("head_out_added")
        keys_current = [sem(f"keys_current{i}") for i in range(2)]
        wq_current = sem("wq_current")
        out_stored = sem("out_stored")

        block = ctx.enter_context(nc.Block())

        xv = x.rearrange("b (t p) d -> p (b t) d", p=P)
        ov = out.rearrange("b (t p) d -> p (b t) d", p=P)

        def run_heads(eng, head, experts):
            head(0, 0, first=True)
            head(1, 1, second=True)
            with eng.Fori(1, SPLIT) as j:
                head(j * 2, 0)
                head(j * 2 + 1, 1)
            experts()
            with eng.Fori(SPLIT, PAIRS - 1) as j:
                head(j * 2, 0, late=j - SPLIT)
                head(j * 2 + 1, 1, late=j - SPLIT)
            head(NHEADS - 2, 0, ahead=1)
            head(NHEADS - 1, 1, ahead=0)

        def over_tiles(eng, tile, first=0):
            for i in range(first, 2):
                tile(i, i)
            with eng.Fori(1, NTILES // 2 - 1) as j:
                tile(j * 2, 0)
                tile(j * 2 + 1, 1)
            tile(NTILES - 3, 0)
            tile(NTILES - 2, 1)
            tile(NTILES - 1, 0)

        @block.sync
        def _(sp):
            def load_x(b):
                here = slice(b * KT, (b + 1) * KT)
                sp.dma_start(acc[:, here, :], xv[:, here, :]).then_inc(x_loaded[b], 16)
            sp.dma_start(up_w, up).then_inc(up_loaded, 16)
            load_x(0)
            sp.dma_start(packed_w[:, :], weights).then_inc(weights_loaded, 16)
            load_x(1)
            sp.dma_start(wo_sb[:, :, :], wo.rearrange("(h k) d -> k h d", k=DK)).then_inc(wo_loaded, 16)
            load_x(2)
            load_x(3)
            sp.dma_start(packed_c[:, :], consts).then_inc(consts_loaded, 16)

            def move_max(n, c, parity):
                sp.wait_ge(mrow_ready, n * 2 + (c + 1))
                sp.dma_start(q_h1[ROW_MAX:ROW_MAX + 1, parity, c * QC:(c + 1) * QC].bitcast(FP32),
                             mrow[:, c, :].bitcast(FP32)).then_inc(mrow_moved[c], 16)

            def expert(i):
                return sp.value_load(expert_of[0:1, bass.ds(i, 1)], min_val=0, max_val=E - 1)

            def load_w1(i, parity):
                if not (isinstance(i, int) and i < 2):
                    sp.wait_ge(w1_split, i - 1)
                sp.dma_start(w1_t[:, parity, :], w1[bass.ds(expert(i), 1), :, :].rearrange("a d f -> d (a f)"))\
                    .then_inc(w1_in[parity], 16)

            def load_tile(i, parity):
                first = isinstance(i, int) and i < 2
                if not first:
                    sp.wait_ge(xgT_ready, i - 1)
                sp.dma_start(xg[:, parity, :, :],
                             xs_dram[bass.ds(i * SLOTS, SLOTS), :].rearrange("(a p) d -> p a d", p=P))\
                    .then_inc(x_in[parity], 16)
                if not (isinstance(i, int) and i == NTILES - 1):
                    load_w1(i + 1, 1 - parity)
                e = expert(i)
                if not first:
                    sp.wait_ge(yT_copied, i - 1)
                sp.dma_start(w2_t[:, parity, :].rearrange("p (a d) -> p a d", a=FT),
                             w2[bass.ds(e, 1), :, :].rearrange("o (a p) d -> p (o a) d", p=P))\
                    .then_inc(w2_in[parity], 16)
                sp.dma_start(b12_t[:, parity, :], b12[bass.ds(e, 1), :, :].rearrange("o p a -> p (o a)"))\
                    .then_inc(b_in[parity], 16)

            sp.wait_ge(zeros_made, 1)
            zeros = row_st[:, 0, :].unsqueeze(1).to_broadcast([P, NTILES * SLOTS // P, D])
            sp.dma_start(xs_dram.rearrange("(t p) d -> p t d", p=P), zeros).then_inc(zeros_stored, 16)

            def keys(g, parity):
                if g < 2:
                    sp.wait_ge(ones_set, 2)
                    sp.wait_ge(k_low, NC)
                    sp.wait_ge(c_copied, NC)
                else:
                    sp.wait_ge(context_added, g * 8 - 8)
                b = g // H
                for dst, src in ((k_hh_cur, k_hh), (k_l1_cur, k_l1)):
                    sp.dma_start(dst[:, parity, :].bitcast(FP32), src[:, b * S:(b + 1) * S].bitcast(FP32))\
                        .then_inc(keys_current[parity], 16)
                sp.dma_start(ckv_cur[:, parity, :], ckv[:, b * KT:(b + 1) * KT, :].rearrange("p t c -> p (t c)"))\
                    .then_inc(keys_current[parity], 16)

            def move_pair(j, new_batch=False):
                for parity in range(2):
                    if new_batch:
                        keys(j * 2 + parity, parity)
                    for c in range(NC):
                        move_max(j * 2 + parity, c, parity)

            def move_pairs(lo, hi):
                while lo < hi:
                    if lo % (H // 2) == 0:
                        move_pair(lo, True)
                        lo += 1
                    else:
                        end = min(hi, (lo // (H // 2) + 1) * (H // 2))
                        with sp.Fori(lo, end) as j:
                            move_pair(j)
                        lo = end

            move_pairs(0, SPLIT - 1)
            for k in range(TOPK):
                sp.wait_ge(rows_sent_k[k], 16 * NT)
            sp.wait_ge(routed, 1)
            load_w1(0, 0)
            load_tile(0, 0)
            move_pairs(SPLIT - 1, SPLIT)
            move_max(2 * SPLIT, 0, 0)
            over_tiles(sp, load_tile, first=1)
            move_max(2 * SPLIT, 1, 0)
            move_max(2 * SPLIT + 1, 0, 1)
            move_max(2 * SPLIT + 1, 1, 1)
            move_pairs(SPLIT + 1, PAIRS)
            def store(lo, hi):
                sp.dma_start(ov[:, lo:hi, :], acc[:, lo:hi, :]).then_inc(out_stored, 16)
            sp.wait_ge(rows_added, PAIRS - SPLIT - 1)
            sp.wait_ge(head_out_added, 4 * (NHEADS - H))
            store(0, NT - KT)
            sp.wait_ge(head_out_added, 4 * NHEADS - 2)
            store(NT - KT, NT - KT // 2)
            sp.wait_ge(head_out_added, 4 * NHEADS)
            store(NT - KT // 2, NT)
            sp.wait_ge(out_stored, 3 * 16)

        @block.gpsimd
        def _(pool):
            steps = [0]

            def link(ins):
                steps[0] += 1
                ins.then_inc(pool_done, 1)
                pool.wait_ge(pool_done, steps[0])
            link(pool.memset(spare[:, :], 0.0))
            pool.memset(prep[:, 0:2, :], 0.0).then_inc(prep_zeroed, 1)
            link(pool.memset(wq_cur[:, :, :].bitcast(FP32), 0.0))
            link(pool.memset(k_h1[KD:P, :].bitcast(FP32), 1.0))
            pool.memset(ckv[:, :, ONE:CW], 1.0).then_inc(ones_set, 1)
            pool.wait_ge(ones_set, 1)
            pool.memset(k_l1[KD:P, :].bitcast(FP32), 1.0).then_inc(ones_set, 1)
            pool.wait_ge(ones_set, 2)
            pool.memset(row_st[:, 0, :], 0.0).then_inc(zeros_made, 1)
            pool.wait_ge(zeros_made, 1)

            def query_weights(n, parity, first=False):
                pool.wait_ge(wq_made, 1)
                if not first:
                    pool.wait_ge(q_ready, n * 2 - 2)
                src = wq_abs[:, bass.ds(n % H, 1), :].rearrange("p a k -> p (a k)")
                pool.tensor_copy(wq_cur[:, parity, 0:KD + 1], src).then_inc(wq_current, 1)

            query_weights(0, 0, True)
            query_weights(1, 1, True)
            for b in range(1, B):
                pool.wait_ge(rstd_ready, b + 1)
                for t in range(max(b * KT, 3 * KT // 2), (b + 1) * KT):
                    if t == 3 * KT // 2 + 3:
                        pool.wait_ge(xn_ready, 3)
                    last = pool.tensor_scalar(xn[:, t, :], acc[:, t, :], mv[:, t, 0:1], rstd[:, 2, t:t + 1],
                                              ALU.subtract, ALU.mult)
                    if t % 4 == 3:
                        last.then_inc(xn_ready, 1)
            query_weights(2, 0)
            pool.wait_ge(xn_ready, NQ)
            pool.wait_ge(consts_loaded, 16)
            pool.tensor_tensor(acc[:, :, :], acc[:, :, :], C["bo"].unsqueeze(1).to_broadcast([P, NT, D]), ALU.add)\
                .then_inc(bo_added, 1)

            def pair(j):
                query_weights(j * 2 + 1, 1)
                if not (isinstance(j, int) and j == PAIRS - 1):
                    query_weights(j * 2 + 2, 0)

            def dispatch(j, first=False):
                for t in range(DISPATCH):
                    for k in range(TOPK):
                        n = j * (DISPATCH * TOPK) + (t * TOPK + k)
                        if not (first and t == 0):
                            pool.wait_ge(routed, 1)
                            pool.wait_ge(rows_sent_k[k], (j * DISPATCH + t) * 16)
                        tt = bass.ds(j * DISPATCH + t, 1)
                        pool.tensor_copy(row_st[:, k, :], xn[:, tt, :].rearrange("p a d -> p (a d)"))\
                            .then_inc(staged, 1)
                        pool.tensor_copy(slot_st[:, k, :], slot_of[:, k, tt]).then_inc(staged, 1)
                        pool.wait_ge(staged, n * 2 + 2)
                        pool.sem_inc(pool_waited, 1)
                        pool.indirect_dma_start(
                            out=xs_dram, out_offset=bass.IndirectOffsetOnAxis(ap=slot_st[:, k, :], axis=0),
                            in_=row_st[:, k, :], in_offset=None).then_inc(rows_sent_k[k], 16)

            pair(1)
            pool.wait_ge(routed, 1)
            pool.wait_ge(zeros_stored, 16)
            dispatch(0, True)
            with pool.Fori(1, NT // DISPATCH - 1) as j:
                pair(j + 1)
                dispatch(j)
            pair(NT // DISPATCH)
            dispatch(NT // DISPATCH - 1)
            with pool.Fori(NT // DISPATCH + 1, SPLIT) as j:
                pair(j)
            pair(SPLIT)

            def store_tile(i, parity):
                pool.wait_ge(y_copied, i + 1)
                pool.dma_start(ys_dram[bass.ds(i * SLOTS, SLOTS), :].rearrange("(a p) d -> p a d", p=P),
                               y_out[:, parity, :, :]).then_inc(y_stored[parity], 16)

            over_tiles(pool, store_tile)
            pool.wait_ge(y_stored[0], (NTILES + 1) // 2 * 16)
            pool.wait_ge(y_stored[1], NTILES // 2 * 16)
            n_staged = NT * TOPK * 2

            def fetch(i):
                if not isinstance(i, int):
                    pool.wait_ge(routed, 1)
                    pool.wait_ge(rows_added, i)
                for t in range(COMBINE):
                    for k in range(TOPK):
                        at = t * TOPK + k
                        last = pool.tensor_copy(slot_st[:, at, :], slot_of[:, k, bass.ds(i * COMBINE + t, 1)])
                        last.then_inc(staged, 1)
                pool.wait_ge(y_stored[0], (NTILES + 1) // 2 * 16)
                pool.wait_ge(staged, i * (COMBINE * TOPK) + (n_staged + COMBINE * TOPK))
                pool.sem_inc(pool_waited, 1)
                for at in range(COMBINE * TOPK):
                    pool.indirect_dma_start(
                        out=fetched[:, at, :], out_offset=None, in_=ys_dram,
                        in_offset=bass.IndirectOffsetOnAxis(ap=slot_st[:, at, :], axis=0)).then_inc(rows_fetched, 16)

            fetch(0)
            with pool.Fori(SPLIT + 1, PAIRS - 1) as j:
                pair(j)
                fetch(j - SPLIT)
            pair(PAIRS - 1)

        @block.scalar
        def _(act):
            def deviations(b):
                act.wait_ge(var_ready, b + 1)
                here = slice(b * KT, (b + 1) * KT)
                act.activation(rstd[:, 0, here], rstd[:, 1, here], ACT.Sqrt).then_inc(std_ready, 1)

            def xT_out(ck):
                act.wait_ge(xT_ready, ck + 1)
                if ck >= 2:
                    act.wait_ge(cg_ready, ck - 1)
                act.activation(xT_st[:, ck % 2, :], sc[0][:, ck % 2 * QC:(ck % 2 + 1) * QC], ACT.Copy)\
                    .then_inc(xT_copied, 1)

            def high_parts(ck):
                here = slice(ck * QC, (ck + 1) * QC)
                act.wait_ge(k_ready, ck + 1)
                act.activation(k_hh[:, here], sc[1][:, 0:QC], ACT.Identity, bias=b_k)
                act.activation(k_h1[0:KD, here], sc[1][0:KD, 0:QC], ACT.Identity, bias=b_k[0:KD])\
                    .then_inc(k_top, 1)
                act.wait_ge(cq_ready, ck + 1)
                act.activation(xq[:, here], sc[1][:, QC:2 * QC], ACT.Identity, bias=b_cq).then_inc(cq_copied, 1)

            def beside(s):
                if 1 <= s < NQ - 1:
                    high_parts(s + 1)
                if s < NQ - 2:
                    xT_out(s + 2)
                if s == 0:
                    deviations(2)
                if s == 2:
                    deviations(3)

            act.wait_ge(prep_zeroed, 1)
            act.activation(spare[:, 1:2], spare[:, 0:1], ACT.Sqrt)
            act.wait_ge(wT_ready, 1)
            pq = mx[:, 0:H * UP].rearrange("p (h k) -> p h k", h=H)
            q3 = uq3.rearrange("p (h k) -> p h k", h=H)
            for g in range(3):
                act.activation(q3[:, :, g * DC:(g + 1) * DC], pq[:, :, 0:DC], ACT.Copy)
            act.activation(q3[:, :, 96:98], pq[:, :, DC:DC + 1].to_broadcast([P, H, 2]), ACT.Copy)
            act.activation(ukT, mx[:, QC:QC + H * UP], ACT.Copy).then_inc(qk_made, 1)
            deviations(0)
            v2 = uv2.rearrange("p (h k) -> p h k", h=H)
            pv = cx[:, 0:H * UP].rearrange("p (h k) -> p h k", h=H)
            act.activation(v2[:, :, 0:UP], pv, ACT.Copy)
            act.activation(v2[:, :, CW:CW + UP], pv, ACT.Copy).then_inc(v2_made, 1)
            act.wait_ge(weights_loaded, 16)
            xT_out(0)
            xT_out(1)
            high_parts(0)
            high_parts(1)
            deviations(1)

            def gelus(i, parity):
                act.wait_ge(b_in[parity], (i // 2) * 16 + 16)
                if not (isinstance(i, int) and i < 2):
                    act.wait_ge(yT_ready, i - 1)
                for f in range(FT):
                    act.wait_ge(hidden_ready, i * FT + (f + 1))
                    act.activation(h_t[parity][:, f * SLOTS:(f + 1) * SLOTS], ps[:, f * 512:f * 512 + SLOTS],
                                   ACT.Gelu, bias=b12_t[:, parity, f:f + 1]).then_inc(hidden_done, 1)

            def experts():
                over_tiles(act, gelus)
                act.activation(spare[:, 1:2], spare[:, 0:1], ACT.Exp)

            def q_one(n, c, parity):
                act.wait_ge(q_ready, n * 2 + (c + 1))
                act.activation(q_h1[:, parity, c * QC:(c + 1) * QC], aux, ACT.Copy).then_inc(q_h1_done, 1)

            def q_high(n, c, parity):
                act.activation(q_hl[0:KD, parity, c * QC:(c + 1) * QC], aux[0:KD], ACT.Copy)\
                    .then_inc(q_hi_done, 1)

            def context_out(g, c, first=False):
                act.wait_ge(context_added, g * 8 + (4 * c + 4))
                if not first:
                    act.wait_ge(head_out_ready, g * 4 + (2 * c - 2))
                act.activation(ctx_sb[:, c, :], cx, ACT.Copy).then_inc(context_copied, 1)

            def head(g, par, attend=True, ahead=2, first=False, second=False, late=None):
                for s in range(8):
                    if attend:
                        act.wait_ge(scores_ready, g * 8 + (s + 1))
                        if not (first and s < 4):
                            act.wait_ge(context_added, g * 8 + (s - 3))
                        act.activation(probs[:, s % 4, :], sc[s % 2], ACT.Exp, scale=SCALE)\
                            .then_inc(probs_ready, 1)
                    if first and s == 3:
                        act.wait_ge(gap_ready, 1)
                        act.activation(first_w[:, 1, :], first_w[:, 0, :], ACT.Exp).then_inc(gap_exp, 1)
                    if s == 0 and attend and not first:
                        context_out(g - 1, 1, second)
                    if s == 4 and attend:
                        context_out(g, 0, first)
                    if s == 1 and ahead >= 1:
                        q_one(g + 1, 1, 1 - par)
                        q_high(g + 1, 1, 1 - par)
                    if s == 5 and ahead >= 2:
                        q_one(g + 2, 0, par)
                        q_high(g + 2, 0, par)
                    if not attend:
                        beside(s)

            q_one(0, 0, 0)
            q_high(0, 0, 0)
            act.wait_ge(prod_ready, 2)
            act.activation(wvo[:, :, 0:D], mx.rearrange("p (h d) -> p h d", h=H), ACT.Copy).then_inc(wvo_made, 1)
            head(-1, 1, attend=False)
            run_heads(act, head, experts)
            context_out(NHEADS - 1, 1)

        @block.vector
        def _(dve):
            steps = [0]

            def link(ins):
                steps[0] += 1
                ins.then_inc(dve_done, 1)
                dve.wait_ge(dve_done, steps[0])

            std, var, r, r3 = (rstd[:, i, :] for i in range(4))

            def statistics(b):
                dve.wait_ge(x_loaded[b], 16)
                here = range(b * KT, (b + 1) * KT)
                for t in here:
                    last = dve.bn_stats(stat[:, t, :], acc[:, t, :])
                link(last)
                for t in here:
                    last = dve.bn_aggr(mv[:, t, :], stat[:, t, :])
                link(last)
                here = slice(b * KT, (b + 1) * KT)
                dve.tensor_scalar(var[:, here], mv[:, here, 1:2].rearrange("p t a -> p (t a)"), EPS, None, ALU.add)\
                    .then_inc(var_ready, 1)

            def inverses(b):
                v, y, e = (rstd[:, i, b * KT:(b + 1) * KT] for i in (1, 2, 3))
                dve.wait_ge(std_ready, b + 1)
                link(dve.reciprocal(y, rstd[:, 0, b * KT:(b + 1) * KT]))
                link(dve.tensor_tensor(e, y, y, ALU.mult))
                link(dve.tensor_tensor(e, e, v, ALU.mult))
                link(dve.tensor_scalar(e, e, -0.5, 1.5, ALU.mult, ALU.add))
                dve.tensor_tensor(y, y, e, ALU.mult).then_inc(rstd_ready, 1)

            def normalise(ck):
                for t in range(ck * 4, ck * 4 + 4):
                    last = dve.tensor_scalar(xn[:, t, :], acc[:, t, :], mv[:, t, 0:1], r[:, t:t + 1],
                                             ALU.subtract, ALU.mult)
                last.then_inc(xn_ready, 1)

            def low_parts(ck):
                here = slice(ck * QC, (ck + 1) * QC)
                dve.wait_ge(k_top, ck + 1)
                dve.scalar_tensor_tensor(k_l1[0:KD, here], sc[1][0:KD, 0:QC], b_k[0:KD],
                                         k_hh[0:KD, here].bitcast(FP32), ALU.add, ALU.subtract)\
                    .then_inc(k_low, 1)
                dve.wait_ge(cq_copied, ck + 1)
                dve.scalar_tensor_tensor(xq[64:96, here], sc[1][64:96, QC:2 * QC], b_cq[64:96],
                                         xq[64:96, here].bitcast(FP32), ALU.add, ALU.subtract)\
                    .then_inc(cq_low, 1)
                dve.wait_ge(cg_ready, ck + 1)
                cg = cx[:, 0:4 * 64].rearrange("p (t k) -> p t k", t=4)
                tiles = slice(ck * 4, ck * 4 + 4)
                dve.tensor_copy(logits[:, tiles, :], cg[:, :, DC:DC + H])
                dve.tensor_tensor(ckv[:, tiles, 0:DC], cg[:, :, 0:DC],
                                  W["bkv"].unsqueeze(1).to_broadcast([P, 4, DC]), ALU.add).then_inc(c_copied, 1)

            def beside(s):
                if s == 0:
                    statistics(2)
                    inverses(2)
                if s == 2:
                    statistics(3)
                if 1 <= s < NQ - 1:
                    low_parts(s + 1)
                if s == 2:
                    inverses(3)

            statistics(0)
            inverses(0)
            dve.wait_ge(rstd_ready, 1)
            normalise(0)
            normalise(1)
            dve.wait_ge(weights_loaded, 16)
            dve.tensor_copy(wvo[:, :, D:OW].rearrange("p h a -> p (h a)"), W["sum_rows"].to_broadcast([P, H]))
            dve.wait_ge(prod_ready, 1)
            f = W["w_q"].rearrange("p (h k) -> p h k", h=H)
            pa = aux[:, 0:H * UP].rearrange("p (h k) -> p h k", h=H)
            dve.tensor_copy(f[:, :, 0:DC], pa[:, :, 0:DC])
            link(dve.tensor_copy(f[:, :, KD:KD + 1], pa[:, :, DC:DC + 1]))
            ff = W["w_q"]
            lo = uq3[:, 0:H * (KD + 1)]
            wqf = wq_abs[:, :, :].rearrange("p h k -> p (h k)")
            link(dve.tensor_copy(wqf, ff))
            link(dve.tensor_tensor(lo, ff, wqf.bitcast(FP32), ALU.subtract))
            link(dve.tensor_scalar(ff, wqf.bitcast(FP32), W["hi_rows"], None, ALU.mult))
            dve.scalar_tensor_tensor(wqf, lo, W["lo_rows"], ff, ALU.mult, ALU.add).then_inc(wq_made, 1)
            dve.wait_ge(ones_set, 1)
            low_parts(0)
            statistics(1)
            low_parts(1)
            inverses(1)

            TE = NT * E
            big = 1.7e38

            def rt(i, n=TE):
                return prep[:, i // 4, (i % 4) * TE:(i % 4) * TE + n]

            def te(v):
                return v.rearrange("p (t e) -> p t e", e=E)

            def over_e(v):
                return v.unsqueeze(2).to_broadcast([P, NT, E])
            one_hot = [rt(0), rt(1)]
            work, rest, both, pre, tot_a, tot_b = (rt(i) for i in range(2, 8))
            small = rt(8)
            best = [small[:, 0:NT], small[:, NT:2 * NT]]
            pick = small[:, 2 * NT:3 * NT]
            fall = C["falling"].unsqueeze(1).to_broadcast([P, NT, E])
            tiles_i = rt(9, E).bitcast(I32)
            cum = [rt(10, E), rt(11, E)]
            tiles = rt(12 - 1, 2 * E)[:, E:2 * E]

            def mark_best(k, src):
                link(dve.reduce_max(best[k], src, AX.X))
                link(dve.tensor_tensor(te(work), src, over_e(best[k]), ALU.is_equal))

            def choose(k):
                link(dve.tensor_tensor(te(work), te(work), fall, ALU.mult))
                link(dve.reduce_max(pick, te(work), AX.X))
                link(dve.tensor_tensor(te(one_hot[k]), fall, over_e(pick), ALU.is_equal))

            def running_sum(src, dst, step, n):
                link(dve.tensor_copy(dst[:, 0:step], src[:, 0:step]))
                link(dve.tensor_tensor(dst[:, step:n], src[:, step:n], src[:, 0:n - step], ALU.add))

            def slots(k):
                link(dve.tensor_tensor(work, one_hot[k], pre, ALU.mult))
                link(dve.reduce_sum(pick, te(work), AX.X))
                return dve.tensor_copy(slot_of[:, k, :], pick)

            def route(step):
                if step == 0:
                    dve.wait_ge(wvo_made, 1)
                    dve.wait_ge(consts_loaded, 16)
                    dve.wait_ge(c_copied, NQ)
                    mark_best(0, logits[:, :, :])
                    choose(0)
                if step == 1:
                    link(dve.tensor_scalar(work, one_hot[0], -2 * big, big, ALU.mult, ALU.add))
                    link(dve.tensor_tensor(te(rest), logits[:, :, :], te(work), ALU.min))
                    mark_best(1, te(rest))
                if step == 2:
                    choose(1)
                    dve.tensor_tensor(both, one_hot[0], one_hot[1], ALU.add).then_inc(chosen, 1)
                    dve.tensor_tensor(first_w[:, 0, :], best[1], best[0], ALU.subtract).then_inc(gap_ready, 1)
                if step == 4:
                    dve.wait_ge(counted, 1)
                    link(dve.tensor_copy(pre, aux[:, 0:TE]))
                    dve.tensor_copy(tot_a, aux[:, TE:2 * TE]).then_inc(counts_taken, 1)
                    dve.wait_ge(counts_taken, 1)
                if step == 5:
                    dve.wait_ge(gap_exp, 1)
                    link(dve.tensor_scalar(best[0], first_w[:, 1, :], 1.0, None, ALU.add))
                    link(dve.reciprocal(first_w[:, 0, :], best[0]))
                    link(dve.tensor_tensor(first_w[:, 1, :], first_w[:, 1, :], first_w[:, 0, :], ALU.mult))
                if step == 6:
                    link(dve.tensor_tensor(pre, pre, tot_a, ALU.subtract))
                    running_sum(tot_a, tot_b, E, TE)
                if step == 7:
                    running_sum(tot_b, tot_a, 2 * E, TE)
                    running_sum(tot_a, tot_b, 4 * E, TE)
                if step == 8:
                    running_sum(tot_b, tot_a, 8 * E, TE)
                    running_sum(tot_a, tot_b, 16 * E, TE)
                if step == 9:
                    link(dve.tensor_tensor(pre, pre, tot_b, ALU.add))
                    link(dve.tensor_scalar(cum[0], tot_b[:, TE - E:TE], float(SLOTS - 1), None, ALU.add))
                    link(dve.tensor_copy(tiles_i, cum[0]))
                    link(dve.tensor_scalar(tiles_i, tiles_i, SLOTS.bit_length() - 1, None, ALU.arith_shift_right))
                if step == 10:
                    link(dve.tensor_copy(cum[0], tiles_i))
                    link(dve.tensor_copy(tiles, cum[0]))
                    running_sum(cum[0], cum[1], 1, E)
                    running_sum(cum[1], cum[0], 2, E)
                    running_sum(cum[0], cum[1], 4, E)
                if step == 11:
                    cmp_ = fetched[:, 0:3, :].rearrange("p a d -> p (a d)")[:, 0:NTILES * E]\
                        .rearrange("p (t e) -> p t e", e=E)
                    link(dve.tensor_tensor(cmp_, C["tile_no"].unsqueeze(2).to_broadcast([P, NTILES, E]),
                                           cum[1].unsqueeze(1).to_broadcast([P, NTILES, E]), ALU.is_ge))
                    link(dve.reduce_sum(work[:, 0:NTILES], cmp_, AX.X))
                    link(dve.tensor_scalar(expert_of[:, :], work[:, 0:NTILES], float(E - 1), None, ALU.min))
                if step == 12:
                    first_slot = rest[:, 0:E]
                    link(dve.tensor_tensor(first_slot, cum[1], tiles, ALU.subtract))
                    link(dve.tensor_scalar(first_slot, first_slot, float(SLOTS), None, ALU.mult))
                    link(dve.tensor_tensor(te(pre), te(pre), first_slot.unsqueeze(1).to_broadcast([P, NT, E]), ALU.add))
                if step == 13:
                    link(slots(0))
                if step == 14:
                    slots(1).then_inc(routed, 1)

            def slots_transposed(i, parity):
                dve.wait_ge(xgT_ready, i + 1)
                dve.tensor_copy(xgT[:, parity, 0, :], mx[:, 0:SLOTS]).then_inc(xgT_high, 1)
                dve.wait_ge(xgT_high, i + 1)
                dve.tensor_tensor(xgT[:, parity, 1, :], mx[:, 0:SLOTS], xgT[:, parity, 0, :].bitcast(FP32),
                                  ALU.subtract).then_inc(xgT_copied, 1)

            def split_w1(i, parity):
                dve.wait_ge(w1_in[parity], (i // 2) * 16 + 16)
                if not (isinstance(i, int) and i < 2):
                    dve.wait_ge(hidden_ready, i * FT - FT)
                dve.tensor_copy(w1_hl[:, parity, 0, :], w1_t[:, parity, :]).then_inc(w1_high, 1)
                dve.wait_ge(w1_high, i + 1)
                dve.tensor_tensor(w1_hl[:, parity, 1, :], w1_t[:, parity, :], w1_hl[:, parity, 0, :].bitcast(FP32),
                                  ALU.subtract).then_inc(w1_split, 1)

            def outputs(i, parity):
                dve.wait_ge(yT_ready, i + 1)
                if not (isinstance(i, int) and i == 0):
                    dve.wait_ge(y_ready, i)
                dve.tensor_scalar(yT, mx[:, 512:512 + SLOTS], b12_t[:, parity, FT:FT + 1], None, ALU.add)\
                    .then_inc(yT_copied, 1)
                if not (isinstance(i, int) and i + 2 >= NTILES):
                    split_w1(i + 2, parity)
                dve.wait_ge(y_ready, i + 1)
                if not (isinstance(i, int) and i < 2):
                    dve.wait_ge(y_stored[parity], (i // 2) * 16)
                dve.tensor_copy(y_out[:, parity, :, :].rearrange("p a d -> p (a d)"), aux[:, 0:SLOTS])\
                    .then_inc(y_copied, 1)

            def experts():
                def tile(i, parity):
                    if not (isinstance(i, int) and i == NTILES - 1):
                        slots_transposed(i + 1, 1 - parity)
                    outputs(i, parity)
                split_w1(0, 0)
                slots_transposed(0, 0)
                split_w1(1, 1)
                over_tiles(dve, tile)

            def add_experts(i, k):
                if k:
                    dve.wait_ge(half_added, i + 1)
                else:
                    dve.wait_ge(rows_fetched, i * (16 * COMBINE * TOPK) + 16 * COMBINE * TOPK)
                for t in range(COMBINE):
                    tt = bass.ds(i * COMBINE + t, 1)
                    a = acc[:, tt, :].rearrange("p a d -> p (a d)")
                    last = dve.scalar_tensor_tensor(a, fetched[:, t * TOPK + k, :], first_w[:, k, tt], a,
                                                    ALU.mult, ALU.add)
                last.then_inc(rows_added if k else half_added, 1)

            def q_low(n, c, parity):
                dve.wait_ge(q_hi_done, n * 2 + (c + 1))
                here = slice(c * QC, (c + 1) * QC)
                dve.tensor_tensor(q_hl[KD:P, parity, here], aux[0:KD, :], q_hl[0:KD, parity, here].bitcast(FP32),
                                  ALU.subtract).then_inc(q_lo_done, 1)

            def add_out(g, c, half, bank=aux):
                dve.wait_ge(head_out_ready, g * 4 + (2 * c + half + 1))
                o = bank[:, 0:2 * OW].rearrange("p (t k) -> p t k", t=2)
                dve.reciprocal(rsum[:, half, :], o[:, :, D:OW].rearrange("p t a -> p (t a)")).then_inc(recip_done, 1)
                dve.wait_ge(recip_done, g * 4 + (2 * c + half + 1))
                b = g // H
                for t in range(2):
                    a = acc[:, bass.ds(b * KT + (c * 4 + half * 2 + t), 1), :].rearrange("p a d -> p (a d)")
                    last = dve.scalar_tensor_tensor(a, o[:, t, 0:D], rsum[:, half, t:t + 1], a, ALU.mult, ALU.add)
                last.then_inc(head_out_added, 1)

            def max_rows(n, c, first=False):
                dve.wait_ge(maxT_ready, n * 2 + (c + 1))
                if not first:
                    dve.wait_ge(mrow_moved[c], n * 16)
                dve.tensor_scalar(mrow[:, c, :], mx[0:4, 0:P], -1.0, None, ALU.mult).then_inc(mrow_ready, 1)

            def head(g, par, attend=True, ahead=2, first=False, second=False, late=None):
                for s in range(8):
                    if s == 0 and attend:
                        max_rows(g, 1, first)
                    if s == 0 and first:
                        route(0)
                    if s == 4 and ahead >= 1:
                        max_rows(g + 1, 0, not attend)
                    if attend and not first:
                        if s == 0:
                            add_out(g - 1, 0, 1)
                        if s in (3, 4):
                            add_out(g - 1, 1, s - 3)
                    if s == 2 and ahead >= 1:
                        q_low(g + 1, 1, 1 - par)
                    if s == 6 and ahead >= 2:
                        q_low(g + 2, 0, par)
                    if s == 7 and attend:
                        if first:
                            dve.wait_ge(bo_added, 1)
                        add_out(g, 0, 0)
                    if s in (2, 6) and par == 1 and late is not None:
                        add_experts(late, s // 4)
                    if ahead >= 1:
                        dve.wait_ge(max_ready, g * 8 + (9 + s))
                        dve.reduce_max(mcol[:, 1 - par, s:s + 1], mx, AX.X).then_inc(max_done, 1)
                    if not attend:
                        beside(s)
                    if first or second:
                        route(s + 1 + 8 * second)

            dve.wait_ge(rstd_ready, 2)
            normalise(2)
            q_low(0, 0, 0)
            head(-1, 1, attend=False)
            run_heads(dve, head, experts)
            add_out(NHEADS - 1, 0, 1, mx[:, 0:QC])
            add_out(NHEADS - 1, 1, 0, mx[:, QC:2 * QC])
            add_out(NHEADS - 1, 1, 1)

        @block.tensor
        def _(pe):
            pe.wait_ge(up_loaded, 16)
            for i, dst in enumerate((mx[:, 0:H * UP], mx[:, QC:QC + H * UP], cx[:, 0:H * UP])):
                for h in range(H):
                    at = (i * H + h) * DK
                    last = pe.transpose(dst[:, h * UP:(h + 1) * UP], up_w[:, at:at + DK], up_w[:, 3 * H * DK:])
            last.then_inc(wT_ready, 1)

            def x_transposed(ck):
                pe.wait_ge(xn_ready, ck + 1)
                if ck >= 2:
                    pe.wait_ge(xT_copied, ck - 1)
                for t in range(4):
                    o = ck % 2 * QC + t * P
                    last = pe.transpose(sc[0][:, o:o + P], xn[:, ck * 4 + t, :], ident)
                last.then_inc(xT_ready, 1)

            def latents(ck):
                xT = xT_st[:, ck % 2, :]
                pe.wait_ge(xT_copied, ck + 1)
                if ck > 0:
                    pe.wait_ge(k_low, ck)
                pe.matmul(sc[1][:, 0:QC], w_k2, xT, start=True, stop=True).then_inc(k_ready, 1)
                if ck > 0:
                    pe.wait_ge(cq_low, ck)
                pe.matmul(sc[1][:, QC:2 * QC], w_cq, xT, start=True, stop=True).then_inc(cq_ready, 1)
                if ck > 0:
                    pe.wait_ge(c_copied, ck)
                for t in range(4):
                    last = pe.matmul(cx[:, t * 64:t * 64 + DC + H], xT[:, t * P:(t + 1) * P],
                                     w_cg, start=True, stop=True)
                last.then_inc(cg_ready, 1)

            def beside(s):
                if 1 <= s < NQ - 1:
                    latents(s + 1)
                if s < NQ - 2:
                    x_transposed(s + 2)

            pe.wait_ge(qk_made, 1)
            for h in range(H):
                last = pe.matmul(aux[:, h * UP:(h + 1) * UP], uq3[:, h * P:(h + 1) * P],
                                 ukT[:, h * UP:(h + 1) * UP], start=True, stop=True)
            last.then_inc(prod_ready, 1)
            pe.wait_ge(weights_loaded, 16)
            x_transposed(0)
            x_transposed(1)
            latents(0)
            latents(1)

            def query(n, c, parity):
                pe.wait_ge(wq_current, n + 1)
                pe.matmul(aux, wq_cur[:, parity, :], xq[:, bass.ds((n // H) * S + c * QC, QC)],
                          start=True, stop=True).then_inc(q_ready, 1)

            def head_out(g, c, half, bank=aux):
                h = g % H
                pe.wait_ge(context_copied, g * 2 + (c + 1))
                for t in range(2):
                    i = half * 2 + t
                    last = pe.matmul(bank[:, t * OW:(t + 1) * OW], ctx_sb[:, c, i * P:(i + 1) * P],
                                     wvo[:, bass.ds(h, 1), :].rearrange("p a k -> p (a k)"), start=True, stop=True)
                last.then_inc(head_out_ready, 1)

            def fill(g, s, par, attend, ahead, first):
                before = attend and not first
                if s == 0 and before:
                    pe.wait_ge(head_out_added, g * 4 - 3)
                    head_out(g - 1, 0, 1)
                if s == 1 and ahead >= 1:
                    if before:
                        pe.wait_ge(head_out_added, g * 4 - 2)
                    else:
                        pe.wait_ge(q_lo_done, g * 2 + 3)
                    query(g + 1, 1, 1 - par)
                if s == 3 and first:
                    pe.wait_ge(q_lo_done, g * 2 + 4)
                    pe.wait_ge(consts_loaded, 16)
                    pe.wait_ge(chosen, 1)
                    both = prep[:, 1, 0:NT * E]
                    pe.matmul(aux[:, 0:NT * E], C["upper"], both, start=True, stop=True)
                    pe.matmul(aux[:, NT * E:2 * NT * E], C["ones"], both, start=True, stop=True).then_inc(counted, 1)
                if s == 3 and before:
                    if ahead >= 1:
                        pe.wait_ge(q_lo_done, g * 2 + 4)
                    else:
                        pe.wait_ge(head_out_added, g * 4 - 2)
                    head_out(g - 1, 1, 0)
                if s == 4 and before:
                    pe.wait_ge(head_out_added, g * 4 - 1)
                    head_out(g - 1, 1, 1)
                if s == 5 and ahead >= 2:
                    if before:
                        pe.wait_ge(head_out_added, g * 4)
                    elif first:
                        pe.wait_ge(counts_taken, 1)
                    else:
                        pe.wait_ge(q_lo_done, g * 2 + 4)
                    query(g + 2, 0, par)
                if s == 7 and attend:
                    if ahead >= 2:
                        pe.wait_ge(q_lo_done, g * 2 + 5)
                    else:
                        pe.wait_ge(head_out_added, g * 4)
                    head_out(g, 0, 0)

            def add_context(g, s, par, first_unit=False):
                c, p = s // 4, s % 4
                pe.wait_ge(probs_ready, g * 8 + (s + 1))
                if p == 0 and not first_unit:
                    pe.wait_ge(context_copied, g * 2 + c)
                for i in range(2):
                    kt = 2 * p + i
                    last = pe.matmul(cx[CW * i:CW * (i + 1), :], ckv_cur[:, par, kt * CW:(kt + 1) * CW],
                                     probs[:, s % 4, i * QC:(i + 1) * QC], start=(p == 0), stop=(p == 3))
                last.then_inc(context_added, 1)

            def head(g, par, attend=True, ahead=2, first=False, second=False, late=None):
                for s in range(8):
                    c, p = s // 4, s % 4
                    if attend:
                        if s == 0:
                            pe.wait_ge(keys_current[par], (g // H) * 48 + 48)
                        if p == 0:
                            pe.wait_ge(q_lo_done, g * 2 + (c + 1))
                            pe.wait_ge(mrow_moved[c], g * 16 + 16)
                        if not (first and s < 2):
                            pe.wait_ge(probs_ready, g * 8 + (s - 1))
                        for i in range(2):
                            kt = 2 * p + i
                            o = sc[s % 2][:, i * QC:(i + 1) * QC]
                            pe.matmul(o, k_hh_cur[:, par, kt * P:(kt + 1) * P], q_hl[:, par, c * QC:(c + 1) * QC],
                                      start=True, stop=False)
                            last = pe.matmul(o, k_l1_cur[:, par, kt * P:(kt + 1) * P],
                                             q_h1[:, par, c * QC:(c + 1) * QC], start=False, stop=True)
                        last.then_inc(scores_ready, 1)
                    fill(g, s, par, attend, ahead, first)
                    if s == 0 and attend:
                        transpose_max(g, 1, par)
                    if s == 4 and ahead >= 1:
                        transpose_max(g + 1, 0, 1 - par)
                    if attend:
                        if s > 0:
                            add_context(g, s - 1, par, first and s == 1)
                        elif not first:
                            add_context(g - 1, 7, 1 - par)
                    if ahead >= 1:
                        if s in (0, 4):
                            pe.wait_ge(q_h1_done, g * 2 + (3 + s // 4))
                            if attend or s == 4:
                                pe.wait_ge(mrow_ready, g * 2 + (2 + s // 4))
                        else:
                            pe.wait_ge(max_done, g * 8 + (8 + s))
                        for i in range(2):
                            last = pe.matmul(mx[:, i * QC:(i + 1) * QC], q_h1[:, 1 - par, s * P:(s + 1) * P],
                                             k_h1[:, bass.ds(((g + 1) // H) * S + i * QC, QC)],
                                             start=True, stop=True)
                        last.then_inc(max_ready, 1)
                    if not attend:
                        beside(s)

            def transpose_max(n, c, parity):
                pe.wait_ge(max_done, n * 8 + (4 * c + 4))
                pe.transpose(mx[0:4, 0:P], mcol[:, parity, 4 * c:4 * c + 4], ident).then_inc(maxT_ready, 1)

            def slots_in(i, parity):
                pe.wait_ge(x_in[parity], (i // 2) * 16 + 16)
                if not (isinstance(i, int) and i == 0):
                    pe.wait_ge(xgT_copied, i)
                for a in range(2):
                    last = pe.transpose(mx[:, a * P:(a + 1) * P], xg[:, parity, a, :], ident)
                last.then_inc(xgT_ready, 1)

            def hidden(i, parity):
                pe.wait_ge(w1_split, i + 1)
                pe.wait_ge(xgT_copied, i + 1)
                for f in range(FT):
                    for w, v in ((0, 0), (0, 1), (1, 0)):
                        last = pe.matmul(ps[:, f * 512:f * 512 + SLOTS], w1_hl[:, parity, w, f * P:(f + 1) * P],
                                         xgT[:, parity, v, :], start=(w == v), stop=(w == 1))
                    last.then_inc(hidden_ready, 1)

            def output(i, parity):
                pe.wait_ge(w2_in[parity], (i // 2) * 16 + 16)
                if not (isinstance(i, int) and i == 0):
                    pe.wait_ge(yT_copied, i)
                for f in range(FT):
                    pe.wait_ge(hidden_done, i * FT + (f + 1))
                    last = pe.matmul(mx[:, 512:512 + SLOTS], w2_t[:, parity, f * P:(f + 1) * P],
                                     h_t[parity][:, f * SLOTS:(f + 1) * SLOTS], start=(f == 0), stop=(f == FT - 1))
                last.then_inc(yT_ready, 1)

            def slots_out(i, parity):
                pe.wait_ge(yT_copied, i + 1)
                if not (isinstance(i, int) and i == 0):
                    pe.wait_ge(y_copied, i)
                for a in range(2):
                    last = pe.transpose(aux[:, a * P:(a + 1) * P], yT[:, a * P:(a + 1) * P], ident)
                last.then_inc(y_ready, 1)

            def experts():
                pe.wait_ge(probs_ready, SPLIT * 16)
                pe.wait_ge(max_done, SPLIT * 16 + 8)
                pe.wait_ge(head_out_added, SPLIT * 8 - 3)

                def tile(i, parity):
                    last = isinstance(i, int) and i == NTILES - 1
                    if not last:
                        slots_in(i + 1, 1 - parity)
                    output(i, parity)
                    if not last:
                        hidden(i + 1, 1 - parity)
                    slots_out(i, parity)
                slots_in(0, 0)
                hidden(0, 0)
                over_tiles(pe, tile)
                pe.wait_ge(y_copied, NTILES)

            pe.wait_ge(cq_low, 1)
            query(0, 0, 0)
            pe.wait_ge(wo_loaded, 16)
            pe.wait_ge(v2_made, 1)
            for h in range(H):
                last = pe.matmul(mx[:, h * D:(h + 1) * D], uv2[:, h * P:(h + 1) * P],
                                 wo_sb[:, h, :], start=True, stop=True)
            last.then_inc(prod_ready, 1)
            pe.wait_ge(wvo_made, 1)
            head(-1, 1, attend=False)
            pe.wait_ge(k_low, NQ)
            pe.wait_ge(cq_low, NQ)
            pe.wait_ge(c_copied, NQ)
            run_heads(pe, head, experts)
            last_head = NHEADS - 1
            head_out(last_head, 0, 1, mx[:, 0:QC])
            add_context(last_head, 7, 1)
            head_out(last_head, 1, 0, mx[:, QC:2 * QC])
            pe.wait_ge(head_out_added, 4 * last_head + 1)
            head_out(last_head, 1, 1)


def layout(inputs):
    import numpy as np
    a = {name.split("_", 2)[2]: np.asarray(v) for name, v in inputs.items()}
    f32 = np.float32

    def zeros(rows, cols):
        return np.zeros((rows, cols), f32)

    def rows_marked(*ranges):
        mask = zeros(P, 1)
        for lo, hi in ranges:
            mask[lo:hi] = 1
        return mask
    up = np.concatenate([np.concatenate([a["W_" + n], a["b_" + n][None]]) for n in ("UQ", "UK", "UV")]
                        + [np.eye(DC + 1, dtype=f32)], axis=1)
    key = [a["W_DKV"], a["W_KR"]]
    key_bias = [a["b_DKV"], a["b_KR"]]
    w_qr = np.concatenate([a["W_QR"]] * 3 + [a["b_QR"][None]] * 2)
    w_q = np.zeros((P, H, KD + 1), f32)
    w_q[0:len(w_qr), :, DC:KD] = w_qr.reshape(-1, H, DR)
    w = {
        "ident": np.eye(P, dtype=f32),
        "w_k2": np.concatenate(key + key, axis=1),
        "w_cq": np.concatenate([a["W_DQ"]] * 3 + [zeros(D, P - 3 * DC)], axis=1),
        "w_cg": np.concatenate([a["W_DKV"], a["gate_w"]], axis=1),
        "w_q": w_q.reshape(P, H * (KD + 1)),
        "bkv": np.repeat(a["b_DKV"][None], P, axis=0),
        "b_k": np.concatenate(key_bias + key_bias)[:, None],
        "b_cq": np.concatenate([a["b_DQ"]] * 3 + [np.ones(P - 3 * DC, f32)])[:, None],
        "hi_rows": rows_marked((0, DC), (2 * DC, 3 * DC + 1)),
        "lo_rows": rows_marked((DC, 2 * DC), (3 * DC + 1, 3 * DC + 2)),
        "sum_rows": rows_marked((ONE, ONE + 1), (CW + ONE, CW + ONE + 1)),
    }
    c = {
        "bo": np.repeat(a["b_O"][None], P, axis=0),
        "upper": np.triu(np.ones((P, P), f32), 1),
        "ones": np.ones((P, P), f32),
        "falling": np.repeat(np.arange(E, 0, -1, dtype=f32)[None], P, axis=0),
        "tile_no": np.repeat(np.arange(NTILES, dtype=f32)[None], P, axis=0),
    }
    assert list(w) == list(W_COLS) and list(c) == list(C_COLS)
    b1 = a["b1"].reshape(E, FT, P).transpose(0, 2, 1)
    arrays = {
        "x": a["h_t"], "up": up, "weights": np.concatenate(list(w.values()), axis=1), "wo": a["W_O"],
        "consts": np.concatenate(list(c.values()), axis=1), "w1": a["w1"], "w2": a["w2"],
        "b12": np.concatenate([b1, a["b2"].reshape(E, P, 1)], axis=2),
    }
    return {name: np.ascontiguousarray(v) for name, v in arrays.items()}


def kernel(**inputs):
    import concourse.bacc as bacc
    from concourse.bass_utils import run_bass_kernel_spmd

    nc = bacc.Bacc("TRN2", target_bir_lowering=False, num_devices=1)
    arrays = layout(inputs)
    args = [nc.dram_tensor(name, a.shape, mybir.dt.from_np(a.dtype), kind="ExternalInput").ap()
            for name, a in arrays.items()]
    args.append(nc.dram_tensor("out", (B, S, D), FP32, kind="ExternalOutput").ap())
    moe_transformer_layer(nc, *args)
    r = run_bass_kernel_spmd(nc, [arrays], core_ids=[0])
    return r.results[0]["out"]
```
